# Optimizing a Trainium2 kernel written in Bass

```python
import numpy as np
import jax
import jax.numpy as jnp

def _softmax(x, axis=-1):
    return jax.nn.softmax(x, axis=axis)

def _gelu(x):
    return jax.nn.gelu(x, approximate=True)

def _silu(x):
    return jax.nn.silu(x)

def _sigmoid(x):
    return jax.nn.sigmoid(x)

def _layernorm(x, axis=-1, eps=1e-05):
    m = jnp.mean(x, axis=axis, keepdims=True)
    v = jnp.var(x, axis=axis, keepdims=True)
    return (x - m) / jnp.sqrt(v + eps)

def _scatter_add(tgt, idx, src, axis=0):
    return tgt.at[idx].add(src)

def _segment_sum(src, seg, n):
    return jax.ops.segment_sum(src, seg, n)
kernel_name = 'mk_adj_ffn_d1_adj_r2_06478b'

def setup_inputs(seed: int=0):
    np.random.seed(seed)
    _w = jnp.asarray

    def _rec_inputs():
        import jax
        import jax.numpy as jnp
        _gk = jax.random.key(seed)
        x = -0.0002928 + 1 * jax.random.normal(jax.random.fold_in(_gk, 1), (16, 512, 256), jnp.float32)
        _a = jax.random.bernoulli(jax.random.fold_in(_gk, 2), 0.03125, (16, 512, 512))
        _a = jnp.logical_or(_a, jnp.swapaxes(_a, -1, -2))
        _a = jnp.logical_or(_a, jnp.eye(512, dtype=bool))
        adj = _a.astype(jnp.int32)
        return (x, adj)
    x, adj = _rec_inputs()

    def _L0_gnn_setup():
        import jax, jax.numpy as jnp
        import numpy as np
        B, N, H, NH = (8, 512, 256, 8)
        DK = H // NH
        key = jax.random.key(seed)
        ks = jax.random.split(key, 6)
        x = jax.random.normal(ks[0], (B, N, H), dtype=jnp.float32)
        adj = jax.random.randint(ks[1], (B, N, N), 0, 2, dtype=jnp.int32)
        adj = jnp.maximum(adj, jnp.eye(N, dtype=jnp.int32)[None])
        s = 1.0 / np.sqrt(H)
        Wq = jax.random.normal(ks[2], (H, H), dtype=jnp.float32) * s
        Wk = jax.random.normal(ks[3], (H, H), dtype=jnp.float32) * s
        Wv = jax.random.normal(ks[4], (H, H), dtype=jnp.float32) * s
        Wg = jax.random.normal(ks[5], (H, 2 * H), dtype=jnp.float32) * (1.0 / np.sqrt(2 * H))
        bg = jnp.zeros((H,), dtype=jnp.float32)
        return {'x': x, 'adj': adj, 'Wq': Wq, 'Wk': Wk, 'Wv': Wv, 'Wg': Wg, 'bg': bg}
    _L0_gnn_all = _L0_gnn_setup()
    _L0_gnn_in = {k: v for k, v in _L0_gnn_all.items() if k in ('Wq', 'Wk', 'Wv', 'Wg', 'bg')}
    del _L0_gnn_all

    def _L0_ffn_setup():
        import jax, jax.numpy as jnp
        import numpy as np
        B, T, H = (2, 1024, 256)
        E, K, INTER = (8, 2, 512)
        key = jax.random.key(seed)
        ks = jax.random.split(key, 8)
        s_h = 1.0 / np.sqrt(H)
        s_i = 1.0 / np.sqrt(INTER)
        return {'x': jax.random.normal(ks[0], (B, T, H), dtype=jnp.float32), 'router_w': jax.random.normal(ks[1], (H, E), dtype=jnp.float32) * s_h, 'Wg': jax.random.normal(ks[2], (E, H, INTER), dtype=jnp.float32) * s_h, 'Wu': jax.random.normal(ks[3], (E, H, INTER), dtype=jnp.float32) * s_h, 'Wd': jax.random.normal(ks[4], (E, INTER, H), dtype=jnp.float32) * s_i, 'Sg': jax.random.normal(ks[5], (H, INTER), dtype=jnp.float32) * s_h, 'Su': jax.random.normal(ks[6], (H, INTER), dtype=jnp.float32) * s_h, 'Sd': jax.random.normal(ks[7], (INTER, H), dtype=jnp.float32) * s_i}
    _L0_ffn_all = _L0_ffn_setup()
    _L0_ffn_in = {k: v for k, v in _L0_ffn_all.items() if k in ('router_w', 'Wg', 'Wu', 'Wd', 'Sg', 'Su', 'Sd')}
    del _L0_ffn_all
    return {'x': x, 'adj': adj, 'L0_gnn_Wq': _L0_gnn_in['Wq'], 'L0_gnn_Wk': _L0_gnn_in['Wk'], 'L0_gnn_Wv': _L0_gnn_in['Wv'], 'L0_gnn_Wg': _L0_gnn_in['Wg'], 'L0_gnn_bg': _L0_gnn_in['bg'], 'L0_ffn_router_w': _L0_ffn_in['router_w'], 'L0_ffn_Wg': _L0_ffn_in['Wg'], 'L0_ffn_Wu': _L0_ffn_in['Wu'], 'L0_ffn_Wd': _L0_ffn_in['Wd'], 'L0_ffn_Sg': _L0_ffn_in['Sg'], 'L0_ffn_Su': _L0_ffn_in['Su'], 'L0_ffn_Sd': _L0_ffn_in['Sd']}

def reference(x, adj, L0_gnn_Wq, L0_gnn_Wk, L0_gnn_Wv, L0_gnn_Wg, L0_gnn_bg, L0_ffn_router_w, L0_ffn_Wg, L0_ffn_Wu, L0_ffn_Wd, L0_ffn_Sg, L0_ffn_Su, L0_ffn_Sd):
    import jax
    import jax.numpy as jnp

    def _L0_gnn_ref(x, adj, Wq, Wk, Wv, Wg, bg):
        import jax, jax.numpy as jnp
        import numpy as np
        B, N, H, NH = (8, 512, 256, 8)
        DK = H // NH
        b, n, h = x.shape
        q = (x @ Wq.T).reshape(b, n, NH, DK)
        k = (x @ Wk.T).reshape(b, n, NH, DK)
        v = (x @ Wv.T).reshape(b, n, NH, DK)
        scores = jnp.einsum('bqhd,bkhd->bhqk', q, k) / jnp.sqrt(jnp.float32(DK))
        mask = (adj != 0)[:, None, :, :]
        scores = jnp.where(mask, scores, -jnp.inf)
        attn = jax.nn.softmax(scores, axis=-1)
        c = jnp.einsum('bhqk,bkhd->bqhd', attn, v).reshape(b, n, h)
        gate = jax.nn.sigmoid(jnp.concatenate([c, x], axis=2) @ Wg.T + bg)
        return gate * x + (1.0 - gate) * c

    def _L0_ffn_ref(x, router_w, Wg, Wu, Wd, Sg, Su, Sd):
        import jax, jax.numpy as jnp
        import numpy as np
        B, T, H = (2, 1024, 256)
        E, K, INTER = (8, 2, 512)
        b, t, h = x.shape
        flat = x.reshape(b * t, h)
        n = flat.shape[0]
        full_scores = jax.nn.softmax(flat @ router_w, axis=-1)
        w, idx = jax.lax.top_k(full_scores, K)
        w = w / jnp.sum(w, axis=-1, keepdims=True)
        cw = jnp.zeros((n, E), dtype=flat.dtype).at[jnp.arange(n)[:, None], idx].add(w)
        g = jnp.einsum('nh,ehi->eni', flat, Wg)
        u = jnp.einsum('nh,ehi->eni', flat, Wu)
        y = jnp.einsum('eni,eih->enh', jax.nn.silu(g) * u, Wd)
        out = jnp.einsum('ne,enh->nh', cw, y)
        out = out + jax.nn.silu(flat @ Sg) * (flat @ Su) @ Sd
        return out.reshape(b, t, h)
    x = x + _L0_gnn_ref(_layernorm(x, axis=-1), adj, L0_gnn_Wq, L0_gnn_Wk, L0_gnn_Wv, L0_gnn_Wg, L0_gnn_bg)
    x = x + _L0_ffn_ref(_layernorm(x, axis=-1), L0_ffn_router_w, L0_ffn_Wg, L0_ffn_Wu, L0_ffn_Wd, L0_ffn_Sg, L0_ffn_Su, L0_ffn_Sd)
    return x

_drawn_inputs = setup_inputs


def setup_inputs(seed=0):
    import zlib

    import numpy as np

    out = dict(_drawn_inputs(seed))
    spreads = {'L0_gnn_bg': (0.0, 0.27)}
    factors = {}
    for name, (base, spread) in spreads.items():
        noise = np.random.default_rng([zlib.crc32(name.encode()), seed]).standard_normal(out[name].shape)
        drawn = base * np.exp(spread * noise) if base else spread * noise
        out[name] = jnp.asarray(drawn.astype(out[name].dtype))
    for name, factor in factors.items():
        out[name] = (out[name] * factor).astype(out[name].dtype)
    return out
```

```python
from contextlib import ExitStack

import concourse.bass as bass
from concourse import mybir

P = 128
F32 = mybir.dt.float32
F32R = mybir.dt.float32r
BF16 = mybir.dt.bfloat16
I32 = mybir.dt.int32
U32 = mybir.dt.uint32
ALU = mybir.AluOpType
ACT = mybir.ActivationFunctionType
AX_X = mybir.AxisListType.X

LN_EPS = 1e-5
MASKED = -1e30
BLOCK = 512


def attention_phase(nc, sems, x, adj, wqkv, wgate, bg, router_w, xn_dram, x1_dram, xs_dram, xg_dram,
                    onehot, slot, weight, msum, region):
    NB, N, D = x.shape
    NT = N // P
    NH = 8
    DK = D // NH
    KF = D // P
    HPT = P // DK
    SCALE = float(DK) ** -0.5
    E = router_w.shape[1]
    AHEAD = 3
    LAG = 3
    POS = NH * NT
    VW = 2 * DK + 2

    ctx = ExitStack()
    with ctx:
        def sb(name, shape, dt=F32):
            return ctx.enter_context(nc.sbuf_tensor(name, shape, dt))

        def sem(name):
            return sems.enter_context(nc.semaphore(name))

        banks = [ctx.enter_context(nc.psum_tensor(f"bank{i}", [P, 512], F32)) for i in range(8)]
        S = banks[0:2]
        T = banks[2:4]
        C = banks[4]
        BT = banks[5]
        G = banks[6:8]

        xn = sb("xn", [P, NT, D])
        xp = sb("xp", [P, NT, D])
        xnp = sb("xnp", [P, NT, D])
        adj_i = sb("adj_i", [P, 2, N], I32)
        bias_q = [sb(f"bias_q{s}", [P, NT, N], BF16) for s in range(2)]
        bias_t = [sb(f"bias_t{s}", [P, NT, N], BF16) for s in range(2)]
        xt_h = sb("xt_h", [P, KF, N], F32R)
        xt_l = sb("xt_l", [P, KF, N], F32R)
        gx = [sb(f"gx{s}", [P, NT, D]) for s in range(2)]
        QH, QL, KH, KL = range(4)
        qk = sb("qk", [P, KF, 4, N], F32R)
        stack = sb("stack", [P, NH, 2, N], F32R)
        SR = 3 * DK
        v = [sb(f"v{s}", [P, NT, NH, VW], F32R) for s in range(2)]
        pf = [sb(f"pf{i}", [P, N]) for i in range(4)]
        ph = [sb(f"ph{i}", [P, N], F32R) for i in range(4)]
        pl = [sb(f"pl{i}", [P, N], F32R) for i in range(4)]
        ct = [sb(f"ct{i}", [P, N]) for i in range(2)]
        cb = sb("cb", [P, NH, NT, VW])
        rden = sb("rden", [P, NH, NT])
        c_tok = sb("c_tok", [P, NT, D])
        ct_h = sb("ct_h", [P, KF, N], F32R)
        ct_l = sb("ct_l", [P, KF, N], F32R)
        z = sb("z", [P, NT, D])
        diff = sb("diff", [P, NT, D])
        x1 = sb("x1", [P, NT, D])
        xn2 = sb("xn2", [P, NT, D])
        wqkv_h = sb("wqkv_h", [P, KF, 3 * D], F32R)
        wqkv_l = sb("wqkv_l", [P, KF, 3 * D], F32R)
        wg_h = sb("wg_h", [P, 2 * KF, D], F32R)
        wg_l = sb("wg_l", [P, 2 * KF, D], F32R)
        bgt = sb("bgt", [P, D])
        rw = sb("rw", [P, KF, E])
        ident = sb("ident", [P, P])
        ident_b = sb("ident_b", [P, P], BF16)
        below = sb("below", [P, P], BF16)
        ones_b = sb("ones_b", [P, P], BF16)
        iota_i = sb("iota_i", [P, E], I32)
        iota_e = sb("iota_e", [P, E])
        start_e = sb("start_e", [P, E])
        stats = sb("stats", [P, NT, 6])
        stats2 = sb("stats2", [P, NT, 6])
        mv = sb("mv", [P, NT, 2])
        mv2 = sb("mv2", [P, NT, 2])
        vr = sb("vr", [P, NT])
        vr2 = sb("vr2", [P, NT])
        rstd = sb("rstd", [P, NT])
        rstd2 = sb("rstd2", [P, NT])
        mhalf = sb("mhalf", [P, NT])
        mx = sb("mx", [P, 2, NT])
        mcol = sb("mcol", [P, 2, 2, NT])
        row = sb("row", [2 * NT, 4, P], F32R)
        lg = sb("lg", [P, NT, E])
        mx8 = sb("mx8", [P, NT, 8])
        ix8 = sb("ix8", [P, NT, 8], U32)
        ef = sb("ef", [P, NT, 2])
        mb = sb("mb", [P, NT, E], BF16)
        msd = sb("msd", [P, E])
        posb = sb("posb", [P, NT, E])
        pick = sb("pick", [P, NT, 2, E])
        idx = sb("idx", [P, NT, 2], U32)
        dl = sb("dl", [P, NT])
        el = sb("el", [P, NT])
        ea = sb("ea", [P, NT])

        s_w = sem("s_w")
        s_const = sem("s_const")
        s_set = sem("s_set")
        s_x = sem("s_x")
        s_adj = sem("s_adj")
        s_bias = sem("s_bias")
        s_stat = sem("s_stat")
        s_rstd = sem("s_rstd")
        s_xn = sem("s_xn")
        s_xnst = sem("s_xnst")
        s_xp = sem("s_xp")
        g_full = sem("g_full")
        g_hi = sem("g_hi")
        g_free = sem("g_free")
        s_ref = [sem(f"s_ref{h}") for h in range(NH)]
        s_row = [sem(f"s_row{h}") for h in range(NH)]
        s_full = sem("s_full")
        s_done = sem("s_done")
        s_mcol = sem("s_mcol")
        t_full = sem("t_full")
        p_exp = sem("p_exp")
        p_hi = sem("p_hi")
        p_lo = sem("p_lo")
        pv = sem("pv")
        s_ct = sem("s_ct")
        b_full = sem("b_full")
        b_free = sem("b_free")
        s_norm = sem("s_norm")
        s_z = sem("s_z")
        s_d = sem("s_d")
        s_mix = sem("s_mix")
        s_stat2 = sem("s_stat2")
        s_rstd2 = sem("s_rstd2")
        s_xn2 = sem("s_xn2")
        s_st = sem("s_st")
        s_rt = sem("s_rt")
        s_el = sem("s_el")
        s_scat = sem("s_scat")
        s_rt0 = sem("s_rt0")
        s_lo = sem("s_lo")
        s_half = sem("s_half")

        s_held_pe, s_held_dve, s_held_pool, s_held_sp = (sem(f"s_held_{e}") for e in ("pe", "dve", "pool", "sp"))

        RT_MAX = NT
        RT_IX = RT_MAX + NT
        RT_EF = RT_IX + 1
        RT_OH = RT_EF + 1
        RT_MB = RT_OH + 1
        RT_DL = RT_MB + 1
        RT_MSD = RT_DL + 1
        RT_EA = RT_MSD + 1
        RT_W0 = RT_EA + 1
        RT_W1 = RT_W0 + 1
        RT_MS = RT_W1 + 1
        RT_PICK = RT_MS + 1
        RT_SLOT = RT_PICK + 1
        RT_IDX = RT_SLOT + 1
        RT = RT_IDX

        block = ctx.enter_context(nc.Block())

        x_t = x.rearrange("b (i p) d -> b p i d", p=P)
        adj_t = adj.rearrange("b (i p) n -> b p i n", p=P)
        xn_t = xn_dram.rearrange("(b i p) d -> b p i d", p=P, i=NT)
        x1_t = x1_dram.rearrange("(b i p) d -> b p i d", p=P, i=NT)
        xs_t = xs_dram.rearrange("(b i p) d -> b p i d", p=P, i=NT)

        UNITS = {6: "P0", 7: "P1", 8: "C0", 9: "C1", 10: "Q0", 11: "K0", 12: "Z0", 13: "Z1",
                 14: "Q1", 15: "K1", 16: "V0", 17: "V1", 18: "G0", 19: "M0", 20: "M1", 21: "G1",
                 23: "X0", 24: "X1", 26: "L0", 28: "T0", 31: "R0"}
        ORDER = list(UNITS.values())
        NU = len(ORDER)
        HI = [u for u in ORDER if u[0] in "PQKVC"]
        POST = "CZXLTR"

        def unit(b, name):
            return (b + 1) * NU + ORDER.index(name)

        def bank(par, name):
            return G[(par * NU + ORDER.index(name)) % 2]

        def hi_index(b, name):
            return (b + 1) * len(HI) + HI.index(name)

        def iterations(eng, body):
            body(-1, 0, False, True, False)
            body(0, 1, True, True, False)
            body(1, 0, True, True, True)
            body(2, 1, True, True, True)
            with eng.Fori(1, (NB - 2) // 2) as i:
                body(i * 2 + 1, 0, True, True, True)
                body(i * 2 + 2, 1, True, True, True)
            body(NB - 1, 0, True, False, True)
            body(NB, 1, False, False, True)

        def ahead(b, h, att, pre):
            return (b, h + AHEAD, att) if h + AHEAD < NH else (b + 1, h + AHEAD - NH, pre)

        def behind(b, p, lag, att):
            if p >= lag:
                return b, p - lag, att
            before = att if not isinstance(b, int) else 0 < b <= NB
            return b - 1, p - lag + POS, before

        def f32(t):
            return t.bitcast(F32)

        @block.sync
        def _(sp):
            sp.dma_start(z[:, 0:3, :].rearrange("p i d -> p (i d)").rearrange("p (k n) -> p k n", k=1),
                         wqkv[0:P, :].rearrange("(k p) n -> p k n", p=P)).then_inc(s_w, 16)
            sp.dma_start(diff[:, 0:3, :].rearrange("p i d -> p (i d)").rearrange("p (k n) -> p k n", k=1),
                         wqkv[P:2 * P, :].rearrange("(k p) n -> p k n", p=P)).then_inc(s_w, 16)
            sp.dma_start(x1[:, :, :], wgate.rearrange("(k p) n -> p k n", p=P)).then_inc(s_w, 16)
            sp.dma_start(rw[:, :, :], router_w.rearrange("(k p) e -> p k e", p=P)).then_inc(s_w, 16)
            sp.dma_start(bgt[:, :], bg.rearrange("(o d) -> o d", o=1).to_broadcast([P, D])).then_inc(s_w, 16)

            def body(b, par, att, pre, post):
                B = b + 1
                A = b - 1
                if pre:
                    if not isinstance(B, int) or B > 0:
                        sp.wait_ge(g_full, unit(b - 1, "P1") + 1)
                        sp.wait_ge(s_xnst, B * 16)
                    sp.dma_start(xn[:, :, :], x_t[bass.ds(B, 1)].rearrange("o p i d -> p (o i) d")
                                 if not isinstance(B, int) else x_t[B]).then_inc(s_x, 16)
                    sp.wait_ge(s_bias, B * 2)
                    sp.dma_start(adj_i[:, :, :], (adj_t[B] if isinstance(B, int) else
                                 adj_t[bass.ds(B, 1)].rearrange("o p i n -> p (o i) n"))[:, 0:2]).then_inc(s_adj, 16)
                if post:
                    sp.wait_ge(s_d, A * 2)
                    sp.wait_ge(s_xnst, A * 16 + 16)
                    dyn = not isinstance(A, int)
                    sp.dma_start(xp[:, :, :], x_t[bass.ds(A, 1)].rearrange("o p i d -> p (o i) d")
                                 if dyn else x_t[A]).then_inc(s_xp, 16)
                    sp.dma_start(xnp[:, :, :], xn_t[bass.ds(A, 1)].rearrange("o p i d -> p (o i) d")
                                 if dyn else xn_t[A]).then_inc(s_xp, 16)
                for h in range(NH):
                    if h == 2 and pre:
                        sp.wait_ge(s_xn, B * NT + NT)
                        sp.dma_start(xn_t[B] if isinstance(B, int) else
                                     xn_t[bass.ds(B, 1)].rearrange("o p i d -> p (o i) d"),
                                     xn[:, :, :]).then_inc(s_xnst, 16)
                    if h == 3 and pre:
                        sp.wait_ge(s_bias, B * 2 + 1)
                        sp.dma_start(adj_i[:, :, :], (adj_t[B] if isinstance(B, int) else
                                     adj_t[bass.ds(B, 1)].rearrange("o p i n -> p (o i) n"))[:, 2:4]).then_inc(s_adj, 16)
                    gb, gh, there = ahead(b, h, att, pre)
                    if there:
                        sp.wait_ge(s_done, (gb * NH + gh) * (NT + 1) + NT + 1)
                        sp.dma_start(f32(stack[SR:SR + 2, gh, 0, :]).rearrange("t (i c) -> t i c", c=P),
                                     f32(row[:, gh % 4, :])).then_inc(s_row[gh], 16)
                    for r in {3: [0, 1], 4: [2, 3], 5: [4], 6: [5, 6], 7: [7]}.get(h, []):
                        if not pre:
                            continue
                        if att:
                            sp.wait_ge(t_full, b * POS + r * NT + NT)
                            sp.nop().then_inc(s_held_sp, 1)
                        m, j = r // HPT, r % HPT
                        sp.wait_ge(g_free, unit(b, "K0" if m == 0 else "K1") + 1)
                        for rows, (a, c) in enumerate([(QH, KH), (QL, KH), (QH, KL)]):
                            sp.dma_start(f32(stack[DK * rows:DK * rows + DK, r, :, :]),
                                         f32(qk[DK * j:DK * j + DK, m, a:c + 1:c - a, :])).then_inc(s_ref[r], 16)
                    if h == 6 and post:
                        dyn = not isinstance(A, int)
                        sp.wait_ge(s_mix, A * 2 + 2)
                        sp.dma_start(x1_t[bass.ds(A, 1)].rearrange("o p i d -> p (o i) d")
                                     if dyn else x1_t[A], x1[:, :, :]).then_inc(s_st, 16)
                        sp.wait_ge(s_xn2, A * NT + NT)
                        sp.dma_start(xs_t[bass.ds(A, 1)].rearrange("o p i d -> p (o i) d")
                                     if dyn else xs_t[A], xn2[:, :, :]).then_inc(s_st, 16)

            iterations(sp, body)
            sp.wait_ge(s_st, NB * 32)

        @block.tensor
        def _(pe):
            pe.wait_ge(s_const, 8)
            pe.wait_ge(s_set, 14)

            def split(out, lh, ll, rh, rl, first, last):
                pe.matmul(out, lh, rh, start=first, stop=False)
                pe.matmul(out, lh, rl, start=False, stop=False)
                return pe.matmul(out, ll, rh, start=False, stop=last)

            def turn(out, src, kf):
                for i in range(NT):
                    last = pe.transpose(out[:, P * i:P * i + P], src[:, i, P * kf:P * kf + P], ident[:, :])
                return last

            def do_unit(b, par, name):
                B, A = b + 1, b - 1
                o = bank(par, name)
                k = int(name[1])
                s = par
                if not (isinstance(b, int) and b == -1 and ORDER.index(name) == 0):
                    pe.wait_ge(g_free, unit(b, name) - 1)
                if name[0] == "P":
                    pe.wait_ge(s_xn, B * NT + NT)
                    last = turn(o, xn, k)
                elif name[0] in "QK":
                    pe.wait_ge(g_free, unit(b, "P1") + 1)
                    c0 = (D if name[0] == "K" else 0) + P * k
                    for kf in range(KF):
                        last = split(o[:, :], wqkv_h[:, kf, c0:c0 + P], wqkv_l[:, kf, c0:c0 + P],
                                     xt_h[:, kf, :], xt_l[:, kf, :], kf == 0, kf == KF - 1)
                elif name[0] in "VG":
                    for ii in range(2):
                        i = 2 * k + ii
                        for kf in range(KF):
                            wh, wl = ((wqkv_h[:, kf, 2 * D:], wqkv_l[:, kf, 2 * D:]) if name[0] == "V" else
                                      (wg_h[:, KF + kf, :], wg_l[:, KF + kf, :]))
                            last = split(o[:, D * ii:D * ii + D], xt_h[:, kf, P * i:P * i + P],
                                         xt_l[:, kf, P * i:P * i + P], wh, wl, kf == 0, kf == KF - 1)
                elif name[0] == "M":
                    pe.wait_ge(s_bias, B * 2 + 2)
                    ob = o[:, :].bitcast(BF16)
                    for kk in range(2):
                        for i in range(NT):
                            kt = 2 * k + kk
                            last = pe.transpose(ob[:, N * kk + P * i:N * kk + P * i + P],
                                                bias_q[s][:, i, P * kt:P * kt + P], ident_b[:, :])
                elif name[0] == "C":
                    pe.wait_ge(s_norm, A * 6 + 6)
                    last = turn(o, c_tok, k)
                elif name[0] == "Z":
                    pe.wait_ge(g_free, unit(b, "C1") + 1)
                    for ii in range(2):
                        i = 2 * k + ii
                        for kf in range(KF):
                            last = split(o[:, D * ii:D * ii + D], ct_h[:, kf, P * i:P * i + P],
                                         ct_l[:, kf, P * i:P * i + P], wg_h[:, kf, :], wg_l[:, kf, :],
                                         kf == 0, kf == KF - 1)
                elif name[0] == "X":
                    pe.wait_ge(s_xn2, A * NT + NT)
                    last = turn(o, xn2, k)
                elif name[0] == "L":
                    pe.wait_ge(g_free, unit(b, "X1") + 1)
                    zt = z[:, :, :].rearrange("p i d -> p (i d)")
                    for kf in range(KF):
                        last = pe.matmul(o[0:E, :], rw[:, kf, :], zt[:, N * kf:N * kf + N],
                                         start=kf == 0, stop=kf == KF - 1)
                elif name[0] == "T":
                    pe.wait_ge(g_free, unit(b, "L0") + 1)
                    pe.nop().then_inc(s_held_pe, 1)
                    lgt = diff[:, :, :].rearrange("p i d -> p (i d)")
                    for i in range(NT):
                        last = pe.transpose(o[:, E * i:E * i + E], lgt[0:E, P * i:P * i + P], ident[0:E, 0:E])
                elif name[0] == "R":
                    pe.wait_ge(s_rt, A * RT + RT_MB)
                    for i in range(NT):
                        pe.matmul(o[:, E * i:E * i + E], below[:, :], mb[:, i, :], start=True, stop=False)
                        for j in range(i):
                            pe.matmul(o[:, E * i:E * i + E], ones_b[:, :], mb[:, j, :], start=False, stop=False)
                        last = pe.matmul(o[:, E * i:E * i + E], ones_b[:, :], msum[:, :], start=False, stop=True)
                last.then_inc(g_full, 1)

            def body(b, par, att, pre, post):
                here = 1 - par
                for h in range(NH):
                    for t in range(NT):
                        p = h * NT + t
                        if att:
                            n = b * POS + p
                            if t == 0:
                                pe.wait_ge(s_row[h], b * 16 + 16)
                            if p == 0:
                                pe.wait_ge(g_free, unit(b - 1, "M1") + 1)
                            if not isinstance(b, int) or b > 0 or p >= 2:
                                pe.wait_ge(p_exp, n - 1)
                            o = T[p % 2]
                            pe.matmul(o[:, :], stack[0:SR + 2, h, 1, P * t:P * t + P], stack[0:SR + 2, h, 0, :],
                                      start=True, stop=False)
                            pe.matmul(o[:, :], ident_b[:, :], bias_t[here][:, t, :],
                                      start=False, stop=True).then_inc(t_full, 1)
                        gb, gh, there = ahead(b, h, att, pre)
                        if there:
                            g5 = (gb * NH + gh) * (NT + 1)
                            first = isinstance(gb, int) and gb == 0 and gh == 0
                            for i in {0: [0, 1], 1: [2, 3]}.get(t, []):
                                if i == 0:
                                    pe.wait_ge(s_ref[gh], gb * 48 + 48)
                                if not first or i >= 2:
                                    pe.wait_ge(s_done, g5 + i - 1)
                                pe.matmul(S[(gh * (NT + 1) + i) % 2][:, :], stack[0:SR, gh, 0, P * i:P * i + P],
                                          stack[0:SR, gh, 1, :], start=True, stop=True).then_inc(s_full, 1)
                            if t == NT - 1:
                                pe.wait_ge(s_mcol, (gb * NH + gh) * 2 + 2)
                                pe.wait_ge(s_done, g5 + NT - 1)
                                pe.transpose(S[(gh * (NT + 1) + NT) % 2][0:2 * NT, 0:P],
                                             mcol[:, gh % 2, :, :].rearrange("p t i -> p (t i)"),
                                             ident[:, :]).then_inc(s_full, 1)
                        if p in UNITS:
                            name = UNITS[p]
                            if (post if name[0] in POST else pre):
                                do_unit(b, par, name)
                            else:
                                pe.wait_ge(g_full, unit(b, name))
                                pe.nop().then_inc(g_full, 1)
                        eb, ep, was = behind(b, p, LAG, att)
                        if was:
                            eh, et = ep // NT, ep % NT
                            vs = v[here if ep <= p else par]
                            if ep == 0:
                                pe.wait_ge(g_free, unit(eb - 1, "V1") + 1)
                            if et == 0 and not (isinstance(eb, int) and eb == 0 and eh == 0):
                                pe.wait_ge(s_ct, eb * NH + eh)
                            pe.wait_ge(p_lo, eb * POS + ep + 1)
                            pe.matmul(C[0:2 * DK + 1, :], vs[:, et, eh, 0:2 * DK + 1], ph[ep % 4][:, :],
                                      start=et == 0, stop=False)
                            pe.matmul(C[0:2 * DK + 1, :], vs[:, et, eh, 0:2 * DK + 1], pl[ep % 4][:, :],
                                      start=False, stop=et == NT - 1).then_inc(pv, 1)
                        eb, ep, was = behind(b, p, 2 * NT, att)
                        if was and t == 0:
                            eh = ep // NT
                            pe.wait_ge(s_ct, eb * NH + eh + 1)
                            pe.wait_ge(b_free, eb * NH + eh)
                            for i in range(NT):
                                last = pe.transpose(BT[:, VW * i:VW * i + 2 * DK + 1],
                                                    ct[eh % 2][0:2 * DK + 1, P * i:P * i + P],
                                                    ident[0:2 * DK + 1, 0:2 * DK + 1])
                            last.then_inc(b_full, 1)

            iterations(pe, body)

        @block.scalar
        def _(act):
            act.wait_ge(s_w, 80)
            zf = z[:, :, :].rearrange("p i d -> p (i d)")
            df = diff[:, :, :].rearrange("p i d -> p (i d)")
            act.activation(wqkv_h[:, 0, :], zf[:, 0:3 * D], ACT.Copy).then_inc(s_set, 1)
            act.activation(wqkv_h[:, 1, :], df[:, 0:3 * D], ACT.Copy).then_inc(s_set, 1)
            act.activation(wg_h[:, :, :], x1[:, :, :], ACT.Copy).then_inc(s_set, 1)

            def evacuate(b, par, name):
                B, A = b + 1, b - 1
                o = bank(par, name)
                k = int(name[1])
                act.wait_ge(g_full, unit(b, name) + 1)
                if name[0] in "MXLT":
                    act.wait_ge(g_free, unit(b, name))
                if name[0] == "P":
                    act.activation(xt_h[:, k, :], o[:, :], ACT.Copy).then_inc(g_hi, 1)
                elif name[0] in "QK":
                    if name == "Q0":
                        for h in range(NH):
                            act.wait_ge(s_ref[h], B * 48)
                    act.activation(qk[:, k, QH if name[0] == "Q" else KH, :], o[:, :], ACT.Copy).then_inc(g_hi, 1)
                elif name[0] == "V":
                    if att_before(b):
                        act.wait_ge(pv, b * POS)
                    act.activation(v[par][:, 2 * k:2 * k + 2, :, 0:DK].rearrange("p i h d -> p (i h) d"),
                                   o[:, :].rearrange("p (j d) -> p j d", d=DK), ACT.Copy).then_inc(g_hi, 1)
                elif name[0] == "M":
                    if att_before(b):
                        act.wait_ge(t_full, b * POS)
                    act.activation(bias_t[par][:, 2 * k:2 * k + 2, :], o[:, :].bitcast(BF16).rearrange(
                        "p (i n) -> p i n", n=N), ACT.Copy).then_inc(g_free, 1)
                elif name[0] == "C":
                    act.activation(ct_h[:, k, :], o[:, :], ACT.Copy).then_inc(g_hi, 1)
                elif name[0] == "X":
                    act.wait_ge(s_mix, A * 2 + 1)
                    act.activation(zf[:, N * k:N * k + N], o[:, :], ACT.Copy).then_inc(g_free, 1)
                elif name[0] == "L":
                    act.wait_ge(s_mix, A * 2 + 2)
                    act.activation(df[0:E, 0:N], o[0:E, :], ACT.Copy).then_inc(g_free, 1)
                elif name[0] == "T":
                    act.wait_ge(s_rt, A * RT)
                    act.activation(lg[:, :, :], o[:, 0:NT * E].rearrange("p (i e) -> p i e", e=E),
                                   ACT.Copy).then_inc(g_free, 1)

            def att_before(b):
                return not isinstance(b, int) or b >= 1

            def body(b, par, att, pre, post):
                A = b - 1
                for h in range(NH):
                    for t in range(NT):
                        p = h * NT + t
                        if p - 1 in UNITS:
                            name = UNITS[p - 1]
                            if name[0] in "ZGR":
                                pass
                            elif post if name[0] in POST else pre:
                                evacuate(b, par, name)
                            else:
                                act.wait_ge(g_full, unit(b, name) + 1)
                                if name in HI:
                                    act.wait_ge(g_hi, hi_index(b, name))
                                else:
                                    act.wait_ge(g_free, unit(b, name))
                                act.nop().then_inc(g_hi if name in HI else g_free, 1)
                        if att:
                            n = b * POS + p
                            act.wait_ge(t_full, n + 1)
                            if not isinstance(b, int) or b > 0 or p >= 4:
                                act.wait_ge(p_lo, n - 3)
                            act.activation(pf[p % 4][:, :], T[p % 2][:, :], ACT.Exp, scale=SCALE).then_inc(p_exp, 1)
                        eb, ep, was = behind(b, p, 1, att)
                        if was and ep % 2 == 1:
                            n = eb * POS + ep
                            act.wait_ge(p_exp, n + 1)
                            act.wait_ge(p_hi, n)
                            if not isinstance(eb, int) or eb > 0 or ep >= 4:
                                act.wait_ge(pv, n - 3)
                            act.activation(ph[ep % 4][:, :], pf[ep % 4][:, :], ACT.Copy).then_inc(p_hi, 1)
                        if p == 16 and post:
                            act.wait_ge(g_free, unit(b, "Z1") + 1)
                            act.activation(z[:, :, :], z[:, :, :], ACT.Tanh, scale=0.5).then_inc(s_z, 1)
                        if p == 31 and post:
                            act.wait_ge(s_rt, A * RT + RT_DL)
                            act.activation(el[:, :], dl[:, :], ACT.Exp).then_inc(s_el, 1)
                        eb, ep, was = behind(b, p, NT + LAG - 1, att)
                        if was and t == (NT + LAG - 1) % NT:
                            eh = ep // NT
                            act.wait_ge(pv, eb * POS + eh * NT + NT)
                            if not (isinstance(eb, int) and eb == 0 and eh < 2):
                                act.wait_ge(b_full, eb * NH + eh - 1)
                            act.activation(ct[eh % 2][0:2 * DK + 1, :], C[0:2 * DK + 1, :], ACT.Copy).then_inc(s_ct, 1)
                        eb, ep, was = behind(b, p, 2 * NT + 1, att)
                        if was and t == 1:
                            eh = ep // NT
                            act.wait_ge(b_full, eb * NH + eh + 1)
                            if eh % 4 == 0:
                                act.wait_ge(s_norm, eb * 6)
                            act.activation(cb[:, eh, :, 0:2 * DK + 1],
                                           BT[:, 0:NT * VW].rearrange("p (i w) -> p i w", w=VW)[:, :, 0:2 * DK + 1],
                                           ACT.Copy).then_inc(b_free, 1)

            iterations(act, body)

        @block.vector
        def _(dve):
            zf = z[:, :, :].rearrange("p i d -> p (i d)")
            df = diff[:, :, :].rearrange("p i d -> p (i d)")
            dve.memset(f32(stack[SR:SR + 2, :, 1, :]), 1.0).then_inc(s_set, 1)
            for s in range(2):
                for i in range(NT):
                    dve.memset(f32(v[s][:, i, :, 2 * DK:2 * DK + 2]), 1.0).then_inc(s_set, 1)
            dve.memset(msum[:, :], 0.0).then_inc(s_rt0, 1)
            dve.wait_ge(s_const, 8)
            dve.tensor_copy(iota_e[:, :], iota_i[:, :]).then_inc(s_rt0, 1)
            dve.wait_ge(s_rt0, 2)
            dve.tensor_scalar(start_e[:, :], iota_e[:, :], float(region), None, ALU.mult).then_inc(s_rt0, 1)
            dve.wait_ge(s_set, 12)
            dve.tensor_tensor(wqkv_l[:, 0, :], zf[:, 0:3 * D], f32(wqkv_h[:, 0, :]), ALU.subtract).then_inc(s_lo, 1)
            dve.tensor_tensor(wqkv_l[:, 1, :], df[:, 0:3 * D], f32(wqkv_h[:, 1, :]), ALU.subtract).then_inc(s_lo, 1)
            dve.tensor_tensor(wg_l[:, :, :], x1[:, :, :], f32(wg_h[:, :, :]), ALU.subtract).then_inc(s_lo, 1)
            dve.wait_ge(s_lo, 3)
            dve.wait_ge(s_rt0, 3)
            dve.nop().then_inc(s_set, 2)

            def low(b, par, name):
                B, A = b + 1, b - 1
                o = bank(par, name)
                k = int(name[1])
                if name[0] in "PQKVC":
                    dve.wait_ge(g_hi, hi_index(b, name) + 1)
                else:
                    dve.wait_ge(g_full, unit(b, name) + 1)
                dve.wait_ge(g_free, unit(b, name))
                if name[0] == "P":
                    dve.tensor_tensor(xt_l[:, k, :], o[:, :], f32(xt_h[:, k, :]), ALU.subtract).then_inc(g_free, 1)
                elif name[0] in "QK":
                    hi, lo = (QH, QL) if name[0] == "Q" else (KH, KL)
                    dve.tensor_tensor(qk[:, k, lo, :], o[:, :], f32(qk[:, k, hi, :]), ALU.subtract).then_inc(g_free, 1)
                elif name[0] == "V":
                    vv = v[par][:, 2 * k:2 * k + 2, :, :]
                    dve.tensor_tensor(vv[:, :, :, DK:2 * DK].rearrange("p i h d -> p (i h) d"),
                                      o[:, :].rearrange("p (j d) -> p j d", d=DK),
                                      f32(vv[:, :, :, 0:DK].rearrange("p i h d -> p (i h) d")),
                                      ALU.subtract).then_inc(g_free, 1)
                elif name[0] == "C":
                    dve.tensor_tensor(ct_l[:, k, :], o[:, :], f32(ct_h[:, k, :]), ALU.subtract).then_inc(g_free, 1)
                elif name[0] == "G":
                    dve.tensor_tensor(gx[par][:, 2 * k:2 * k + 2, :], o[:, :].rearrange("p (i d) -> p i d", d=D),
                                      bgt[:, :].rearrange("p (o d) -> p o d", o=1).to_broadcast([P, 2, D]),
                                      ALU.add).then_inc(g_free, 1)
                elif name[0] == "Z":
                    dve.wait_ge(s_rt, A * RT)
                    dve.tensor_tensor(z[:, 2 * k:2 * k + 2, :], o[:, :].rearrange("p (i d) -> p i d", d=D),
                                      gx[par][:, 2 * k:2 * k + 2, :], ALU.add).then_inc(g_free, 1)
                elif name[0] == "R":
                    dve.tensor_tensor(posb[:, :, :], o[:, 0:NT * E].rearrange("p (i e) -> p i e", e=E),
                                      start_e[:, :].rearrange("p (o e) -> p o e", o=1).to_broadcast([P, NT, E]),
                                      ALU.add).then_inc(g_free, 1)

            def skip(b, name):
                if name in HI:
                    dve.wait_ge(g_hi, hi_index(b, name) + 1)
                else:
                    dve.wait_ge(g_full, unit(b, name) + 1)
                dve.wait_ge(g_free, unit(b, name))
                dve.nop().then_inc(g_free, 1)

            def statistics(src, st, s, base):
                dve.wait_ge(s, base)
                for i in range(NT):
                    dve.bn_stats(st[:, i, :], src[:, i, :]).then_inc(s, 1)

            def variance(st, m, va, s, base):
                dve.wait_ge(s, base + NT)
                dve.nop().then_inc(s_held_dve, 1)
                for i in range(NT):
                    dve.bn_aggr(m[:, i, :], st[:, i, :]).then_inc(s, 1)
                dve.wait_ge(s, base + 2 * NT)
                dve.tensor_scalar(va[:, :], m[:, :, 1], LN_EPS, None, ALU.add).then_inc(s, 1)

            def normalise(half, b):
                hs = slice(4 * half, 4 * half + 4)
                base = b * 6 + 3 * half
                dve.wait_ge(b_free, b * NH + 4 * half + 4)
                dve.wait_ge(s_norm, base)
                dve.reciprocal(rden[:, hs, :], cb[:, hs, :, 2 * DK]).then_inc(s_norm, 1)
                cv = c_tok[:, :, :].rearrange("p i (h d) -> p h i d", d=DK)[:, hs]
                dve.tensor_tensor(cv, cb[:, hs, :, 0:DK], cb[:, hs, :, DK:2 * DK], ALU.add).then_inc(s_norm, 1)
                dve.wait_ge(s_norm, base + 2)
                dve.tensor_tensor(cv, cv, rden[:, hs, :].rearrange("p h (i o) -> p h i o", o=1)
                                  .to_broadcast([P, 4, NT, DK]), ALU.mult).then_inc(s_norm, 1)

            def finish_routing(b, par):
                A = b - 1
                rt = A * RT
                wv = weight[:, bmm(A), :].rearrange("p o (i k) -> p (o i) k", k=2)
                dve.wait_ge(s_el, A + 1)
                dve.tensor_scalar(ea[:, :], el[:, :], 1.0, None, ALU.add).then_inc(s_rt, 1)
                dve.wait_ge(s_rt, rt + RT_EA)
                dve.reciprocal(wv[:, :, 0], ea[:, :]).then_inc(s_rt, 1)
                dve.wait_ge(s_rt, rt + RT_W0)
                dve.tensor_tensor(wv[:, :, 1], el[:, :], wv[:, :, 0], ALU.mult).then_inc(s_rt, 1)
                dve.wait_ge(g_full, unit(b, "R0") + 1)
                low(b, par, "R0")
                dve.tensor_tensor(msum[:, :], msum[:, :], msd[:, :], ALU.add).then_inc(s_rt, 1)
                dve.wait_ge(g_free, unit(b, "R0") + 1)
                oh = onehot[:, bmm(A), :, :].rearrange("p o (i k) e -> p (o i) k e", k=2)
                dve.tensor_tensor(pick[:, :, :, :], oh, posb[:, :, :].rearrange("p i (o e) -> p i o e", o=1)
                                  .to_broadcast([P, NT, 2, E]), ALU.mult).then_inc(s_rt, 1)
                dve.wait_ge(s_rt, rt + RT_PICK)
                sv = slot[:, bmm(A), :].rearrange("p o j -> p (o j)")
                dve.tensor_reduce(sv, pick[:, :, :, :].rearrange("p i k e -> p (i k) e"), AX_X,
                                  ALU.add).then_inc(s_rt, 1)
                dve.wait_ge(s_rt, rt + RT_SLOT)
                dve.wait_ge(s_scat, A * 16 * 2 * NT)
                dve.nop().then_inc(s_held_dve, 1)
                dve.tensor_copy(idx[:, :, :].rearrange("p i k -> p (i k)"), sv).then_inc(s_rt, 1)

            def bmm(b):
                return slice(b, b + 1) if isinstance(b, int) else bass.ds(b, 1)

            def body(b, par, att, pre, post):
                B, A = b + 1, b - 1
                for h in range(NH):
                    for t in range(NT):
                        p = h * NT + t
                        if p == 0 and (not isinstance(b, int) or b >= 0):
                            if not isinstance(b, int) or b >= 2:
                                finish_routing(b - 1, 1 - par)
                            else:
                                skip(b - 1, "R0")
                        if p - 2 in UNITS and UNITS[p - 2][0] not in "R":
                            name = UNITS[p - 2]
                            if name[0] in "PQKVCGZ":
                                if post if name[0] in POST else pre:
                                    low(b, par, name)
                                else:
                                    skip(b, name)
                        eb, ep, was = behind(b, p, 1, att)
                        if was and ep % 2 == 0:
                            n = eb * POS + ep
                            dve.wait_ge(p_exp, n + 1)
                            dve.wait_ge(p_hi, n)
                            if not isinstance(eb, int) or eb > 0 or ep >= 4:
                                dve.wait_ge(pv, n - 3)
                            dve.tensor_copy(ph[ep % 4][:, :], pf[ep % 4][:, :]).then_inc(p_hi, 1)
                        gb, gh, there = ahead(b, h, att, pre)
                        if there:
                            gg = gb * NH + gh
                            slot2 = gh % 2
                            bq = bias_q[par if gh < AHEAD and h + AHEAD >= NH else 1 - par]
                            for i in {0: [0, 1], 1: [2, 3]}.get(t, []):
                                dve.wait_ge(s_full, gg * (NT + 1) + i + 1)
                                if i == 0 and gh == 0:
                                    dve.wait_ge(s_bias, gb * 2 + 2)
                                if i == 0 and not (isinstance(gb, int) and gb == 0 and gh < 2):
                                    dve.wait_ge(s_mcol, gg * 2 - 2)
                                o = S[(gh * (NT + 1) + i) % 2]
                                dve.nop().then_inc(s_held_dve, 1)
                                dve.tensor_tensor_reduce(o[:, :], o[:, :], bq[:, i, :], 1.0, 3.0 * MASKED,
                                                         ALU.add, ALU.max, mx[:, slot2, i:i + 1]).then_inc(s_done, 1)
                            if t == 2:
                                dve.wait_ge(s_done, gg * (NT + 1) + NT)
                                if not (isinstance(gb, int) and gb == 0 and gh < 2):
                                    dve.wait_ge(s_done, (gg - 1) * (NT + 1))
                                mc = mcol[:, slot2]
                                dve.tensor_scalar(mc[:, 0, :].bitcast(F32R), mx[:, slot2, :], -1.0, None,
                                                  ALU.mult).then_inc(s_mcol, 1)
                                dve.wait_ge(s_mcol, gg * 2 + 1)
                                dve.scalar_tensor_tensor(out=mc[:, 1, :], in0=mx[:, slot2, :], scalar=-1.0,
                                                         in1=mc[:, 0, :], op0=ALU.mult,
                                                         op1=ALU.subtract).then_inc(s_mcol, 1)
                            if t == 3:
                                dve.wait_ge(s_full, gg * (NT + 1) + NT + 1)
                                if not (isinstance(gb, int) and gb == 0 and gh < 4):
                                    fb = gb if gh >= 4 else gb - 1
                                    dve.wait_ge(s_row[(gh - 4) % NH], fb * 16 + 16)
                                dve.tensor_copy(row[:, gh % 4, :], S[(gh * (NT + 1) + NT) % 2][0:2 * NT, 0:P]
                                                ).then_inc(s_done, 1)
                        if pre and p == 2:
                            dve.wait_ge(s_x, B * 16 + 16)
                            statistics(xn, stats, s_stat, B * (2 * NT + 1))
                        if pre and p == 3:
                            dve.wait_ge(s_xn, B * NT)
                            variance(stats, mv, vr, s_stat, B * (2 * NT + 1))
                        if pre and p == 5:
                            dve.wait_ge(s_rstd, B + 1)
                            for i in range(NT):
                                dve.tensor_scalar(xn[:, i, :], xn[:, i, :], mv[:, i, 0:1], rstd[:, i:i + 1],
                                                  ALU.subtract, ALU.mult).then_inc(s_xn, 1)
                        if p == 6 and ((0 < b <= NB) if isinstance(b, int) else True):
                            normalise(1, A)
                        if p == 24 and att:
                            if post:
                                dve.wait_ge(s_d, A * 2 + 2)
                                dve.wait_ge(g_full, unit(b, "C1") + 1)
                            normalise(0, b)
                        if pre and p in (11, 14):
                            k = 0 if p == 11 else 1
                            dve.wait_ge(s_adj, B * 32 + 16 * k + 16)
                            if not isinstance(b, int) or b >= 1:
                                dve.wait_ge(s_done, b * NH * (NT + 1))
                            dve.tensor_scalar(bias_q[par][:, 2 * k:2 * k + 2, :], adj_i[:, :, :], 0.0, MASKED,
                                              ALU.is_equal, ALU.mult).then_inc(s_bias, 1)
                        if post and p == 17:
                            dve.wait_ge(s_z, A + 1)
                            dve.wait_ge(s_d, A * 2 + 2)
                            dve.scalar_tensor_tensor(out=df[:, :], in0=zf[:, :], scalar=1.0, in1=df[:, :],
                                                     op0=ALU.add, op1=ALU.mult).then_inc(s_mix, 1)
                        if post and p == 18:
                            dve.wait_ge(s_mix, A * 2 + 1)
                            x1f = x1[:, :, :].rearrange("p i d -> p (i d)")
                            dve.scalar_tensor_tensor(out=x1f, in0=df[:, :], scalar=0.5, in1=x1f,
                                                     op0=ALU.mult, op1=ALU.add).then_inc(s_mix, 1)
                        if post and p == 19:
                            dve.wait_ge(s_mix, A * 2 + 2)
                            statistics(x1, stats2, s_stat2, A * (2 * NT + 1))
                        if post and p == 20:
                            dve.wait_ge(s_xn2, A * NT)
                            variance(stats2, mv2, vr2, s_stat2, A * (2 * NT + 1))
                        if post and p == 22:
                            dve.wait_ge(s_rstd2, A + 1)
                            dve.wait_ge(s_scat, A * 16 * 2 * NT)
                            dve.wait_ge(s_st, A * 32)
                            for i in range(NT):
                                dve.tensor_scalar(xn2[:, i, :], x1[:, i, :], mv2[:, i, 0:1], rstd2[:, i:i + 1],
                                                  ALU.subtract, ALU.mult).then_inc(s_xn2, 1)
                        if post and p == 29:
                            rt = A * RT
                            dve.wait_ge(g_free, unit(b, "T0") + 1)
                            dve.wait_ge(s_rt, rt)
                            dve.nop().then_inc(s_held_dve, 1)
                            for i in range(NT):
                                dve.max(mx8[:, i, :], lg[:, i, :]).then_inc(s_rt, 1)
                            dve.wait_ge(s_rt, rt + RT_MAX)
                            dve.nop().then_inc(s_held_dve, 1)
                            for i in range(NT):
                                dve.max_index(ix8[:, i, :], mx8[:, i, :], lg[:, i, :]).then_inc(s_rt, 1)
                            dve.wait_ge(s_rt, rt + RT_IX)
                            dve.tensor_copy(ef[:, :, :], ix8[:, :, 0:2]).then_inc(s_rt, 1)
                        if post and p == 30:
                            rt = A * RT
                            dve.wait_ge(s_rt, rt + RT_EF)
                            oh = onehot[:, bmm(A), :, :].rearrange("p o j e -> p (o j) e")
                            dve.tensor_tensor(oh, ef[:, :, :].rearrange("p i (k o) -> p (i k) o", o=1)
                                              .to_broadcast([P, 2 * NT, E]),
                                              iota_e[:, :].rearrange("p (o e) -> p o e", o=1)
                                              .to_broadcast([P, 2 * NT, E]), ALU.is_equal).then_inc(s_rt, 1)
                            dve.wait_ge(s_rt, rt + RT_OH)
                            ohk = oh.rearrange("p (i k) e -> p i k e", k=2)
                            dve.tensor_tensor(mb[:, :, :], ohk[:, :, 0, :], ohk[:, :, 1, :], ALU.add).then_inc(s_rt, 1)
                            dve.tensor_tensor(dl[:, :], mx8[:, :, 1], mx8[:, :, 0], ALU.subtract).then_inc(s_rt, 1)
                            dve.wait_ge(s_rt, rt + RT_MB)
                            dve.tensor_reduce(msd[:, :], mb[:, :, :].rearrange("p i e -> p e i"), AX_X,
                                              ALU.add).then_inc(s_rt, 1)

            iterations(dve, body)
            finish_routing(NB, (NB + 1) % 2)

        @block.gpsimd
        def _(pool):
            for m in (ident, ident_b):
                pool.memset(m[:, :], 0.0).then_inc(s_const, 1)
            pool.memset(below[:, :], 1.0).then_inc(s_const, 1)
            pool.memset(ones_b[:, :], 1.0).then_inc(s_const, 1)
            pool.memset(mhalf[:, :], -0.5).then_inc(s_half, 1)
            pool.wait_ge(s_const, 4)
            for m in (ident, ident_b):
                pool.affine_select(out=m[:, :], in_=m[:, :], compare_op=ALU.not_equal, fill=1.0, base=0,
                                   pattern=[[-1, P]], channel_multiplier=1).then_inc(s_const, 1)
            pool.affine_select(out=below[:, :], in_=below[:, :], compare_op=ALU.is_gt, fill=0.0, base=0,
                               pattern=[[1, P]], channel_multiplier=-1).then_inc(s_const, 1)
            pool.iota(iota_i[:, :], [[1, E]], base=0, channel_multiplier=0).then_inc(s_const, 1)
            pool.wait_ge(s_half, 1)

            def scatter(A, j):
                if j == 0:
                    pool.wait_ge(s_rt, A * RT + RT_IDX)
                    pool.nop().then_inc(s_held_pool, 1)
                i, k = j // 2, j % 2
                pool.indirect_dma_start(
                    out=xg_dram, out_offset=bass.IndirectOffsetOnAxis(ap=idx[:, i, k:k + 1], axis=0),
                    in_=xn2[:, i, :], in_offset=None).then_inc(s_scat, 16)

            def body(b, par, att, pre, post):
                B, A = b + 1, b - 1
                for p in range(POS):
                    if (b >= 2 if isinstance(b, int) else True) and 5 <= p < 5 + 2 * NT:
                        scatter(b - 2, p - 5)
                    if pre and p == 4:
                        pool.wait_ge(s_stat, B * (2 * NT + 1) + 2 * NT + 1)
                        pool.wait_ge(s_xn, B * NT)
                        pool.tensor_tensor(rstd[:, :], vr[:, :], mhalf[:, :], ALU.pow).then_inc(s_rstd, 1)
                    if post and p in (13, 15):
                        pool.wait_ge(s_norm, A * 6 + 6)
                        pool.wait_ge(s_xp, A * 32 + 32)
                        if p == 13:
                            pool.wait_ge(g_free, (b) * NU)
                            pool.tensor_tensor(diff[:, :, :], xnp[:, :, :], c_tok[:, :, :], ALU.subtract).then_inc(s_d, 1)
                        else:
                            pool.wait_ge(s_st, A * 32)
                            pool.wait_ge(s_xn2, A * NT)
                            pool.tensor_tensor(x1[:, :, :], xp[:, :, :], c_tok[:, :, :], ALU.add).then_inc(s_d, 1)
                    if post and p == 21:
                        pool.wait_ge(s_stat2, A * (2 * NT + 1) + 2 * NT + 1)
                        pool.tensor_tensor(rstd2[:, :], vr2[:, :], mhalf[:, :], ALU.pow).then_inc(s_rstd2, 1)
                    if att:
                        n = b * POS + p
                        pool.wait_ge(p_hi, n + 1)
                        if not isinstance(b, int) or b > 0 or p >= 4:
                            pool.wait_ge(pv, n - 3)
                        pool.tensor_tensor(pl[p % 4][:, :], pf[p % 4][:, :], f32(ph[p % 4][:, :]),
                                           ALU.subtract).then_inc(p_lo, 1)
            iterations(pool, body)
            for j in range(2 * NT):
                scatter(NB - 1, j)
            pool.wait_ge(s_scat, NB * 2 * NT * 16)


def ffn_phase(nc, sems, w_dram, xg_dram, y_dram, onehot, slot, msum, fidx, n_batches, region, experts, inter):
    D = y_dram.shape[1]
    KF = D // P
    MT = inter // P
    NT = BLOCK // P
    NBLK = y_dram.shape[0] // BLOCK
    NE = experts + 1
    GU = 2 * KF * inter
    WC = GU + MT * D
    CH = WC // 3
    assert CH == KF * inter == MT * D
    MAXB = (region - BLOCK) // BLOCK + 1

    ctx = ExitStack()
    with ctx:
        def sb(name, shape, dt=F32):
            return ctx.enter_context(nc.sbuf_tensor(name, shape, dt))

        def sem(name):
            return sems.enter_context(nc.semaphore(name))

        banks = [ctx.enter_context(nc.psum_tensor(f"fbank{i}", [P, 512], F32)) for i in range(8)]
        GB, UB, TB, OB = banks[0:2], banks[2:4], banks[4:6], banks[6:8]

        raw = [sb(f"raw{s}", [P, WC]) for s in range(2)]
        wh = [sb(f"wh{s}", [P, WC], F32R) for s in range(2)]
        wl = [sb(f"wl{s}", [P, WC], F32R) for s in range(2)]
        xb = [sb(f"xb{s}", [P, NT, D]) for s in range(2)]
        xh = [sb(f"xh{s}", [P, KF, BLOCK], F32R) for s in range(2)]
        xl = [sb(f"xl{s}", [P, KF, BLOCK], F32R) for s in range(2)]
        sg = [sb(f"sg{s}", [P, BLOCK]) for s in range(2)]
        am = [sb(f"am{s}", [P, BLOCK]) for s in range(2)]
        ah = [sb(f"ah{s}", [P, MT, BLOCK], F32R) for s in range(2)]
        al = [sb(f"al{s}", [P, MT, BLOCK], F32R) for s in range(2)]
        yb = [sb(f"yb{s}", [P, NT, D]) for s in range(2)]
        fident = sb("fident", [P, P])
        fones = sb("fones", [P, P], BF16)
        zero = sb("zero", [P, D])
        cnt = sb("cnt", [P, experts])
        ki = sb("ki", [P, MAXB], I32)
        kf_ = sb("kf_", [P, MAXB])
        cmp = sb("cmp", [P, experts, MAXB])
        nblk = sb("nblk", [P, NE])
        one9 = sb("one9", [P, NE])
        cum = sb("cum", [P, NE])
        base = sb("base", [P, NE])
        ei = sb("ei", [P, NE], I32)
        ef = sb("eft", [P, NE])
        est = sb("est", [P, NE])
        shift = sb("shift", [P, NE])
        ji = sb("ji", [P, NBLK], I32)
        jf = sb("jf", [P, NBLK])
        ge0 = sb("ge0", [P, NBLK, NE])
        ge1 = sb("ge1", [P, NBLK, NE])
        jr = sb("jr", [P, NBLK])
        rows = sb("rows", [P, NBLK, NE])
        tef = sb("tef", [P, NBLK])
        trf = sb("trf", [P, NBLK])
        tab_e = sb("tab_e", [P, NBLK], I32)
        tab_r = sb("tab_r", [P, NBLK], I32)
        toff = sb("toff", [P, experts, NT], I32)
        tofff = sb("tofff", [P, experts, NT])
        tstart = sb("tstart", [P, experts])
        tidx = sb("tidx", [P, experts, NT], U32)
        shf = sb("shf", [P, 4 * 2 * NT, experts])
        shs = sb("shs", [P, n_batches * 2 * NT])

        s_k = sem("s_k")
        s_cnt = sem("s_cnt")
        s_tb = sem("s_tb")
        s_fx = sem("s_fx")
        s_tail = sem("s_tail")
        s_raw = [sem(f"s_raw{s}") for s in range(2)]
        s_xb = [sem(f"s_xb{s}") for s in range(2)]
        s_yb = [sem(f"s_yb{s}") for s in range(2)]
        s_wh = sem("s_wh")
        s_wl = sem("s_wl")
        x_full = sem("x_full")
        x_hi = sem("x_hi")
        x_lo = sem("x_lo")
        g_full = sem("g_fullb")
        u_full = sem("u_full")
        s_sg = sem("s_sg")
        s_am = sem("s_am")
        s_ah = sem("s_ah")
        s_al = sem("s_al")
        y_full = sem("y_full")
        s_y = [sem(f"s_y{j}") for j in range(2)]

        block = ctx.enter_context(nc.Block())
        x_rows = xg_dram
        PAIRS = (NBLK - 3) // 2
        assert NBLK == 2 * PAIRS + 3
        TB_N = 15

        def blocks(eng, body):
            body(0, 0)
            body(1, 1)
            body(2, 0)
            with eng.Fori(1, PAIRS) as i:
                body(i * 2 + 1, 1)
                body(i * 2 + 2, 0)
            body(NBLK - 2, 1)
            body(NBLK - 1, 0)

        @block.gpsimd
        def _(pool):
            pool.memset(fident[:, :], 0.0).then_inc(s_k, 1)
            pool.memset(fones[:, :], 1.0).then_inc(s_k, 1)
            pool.memset(zero[:, :], 0.0).then_inc(s_k, 1)
            pool.wait_ge(s_k, 3)
            pool.affine_select(out=fident[:, :], in_=fident[:, :], compare_op=ALU.not_equal, fill=1.0, base=0,
                               pattern=[[-1, P]], channel_multiplier=1).then_inc(s_k, 1)
            pool.iota(ki[:, :], [[BLOCK, MAXB]], base=0, channel_multiplier=0).then_inc(s_k, 1)
            pool.iota(ei[:, :], [[1, NE]], base=0, channel_multiplier=0).then_inc(s_k, 1)
            pool.iota(ji[:, :], [[1, NBLK]], base=0, channel_multiplier=0).then_inc(s_k, 1)
            pool.iota(toff[:, :, :], [[0, experts], [P, NT]], base=0, channel_multiplier=1).then_inc(s_k, 1)

            def low(n, s, part):
                pool.wait_ge(s_wh, n * 3 + part + 1)
                c = slice(CH * part, CH * part + CH)
                pool.tensor_tensor(wl[s][:, c], raw[s][:, c], f32(wh[s][:, c]), ALU.subtract).then_inc(s_wl, 1)

            for part in range(3):
                low(0, 0, part)
            pool.wait_ge(s_tb, TB_N)
            for e in range(experts):
                for q in range(NT):
                    pool.indirect_dma_start(
                        out=xg_dram, out_offset=bass.IndirectOffsetOnAxis(ap=tidx[:, e, q:q + 1], axis=0),
                        in_=zero[:, :], in_offset=None).then_inc(s_tail, 16)

            def body(n, s):
                if not isinstance(n, int) or n < NBLK - 1:
                    for part in range(3):
                        low(n + 1, 1 - s, part)

            blocks(pool, body)

        @block.sync
        def _(sp):
            def load(n, s, x_only=False):
                e = sp.value_load(tab_e[0:1, n:n + 1] if isinstance(n, int) else tab_e[0:1, bass.ds(n, 1)],
                                  min_val=0, max_val=experts)
                sp.dma_start(raw[s][:, :], w_dram[bass.ds(e, 1)].rearrange("o p c -> p (o c)")).then_inc(s_raw[s], 16)
                r = sp.value_load(tab_r[0:1, n:n + 1] if isinstance(n, int) else tab_r[0:1, bass.ds(n, 1)],
                                  min_val=0, max_val=x_rows.shape[0] - BLOCK)
                sp.dma_start(xb[s][:, :, :], x_rows[bass.ds(r, BLOCK)].rearrange("(p i) d -> p i d", i=NT)
                             ).then_inc(s_xb[s], 16)

            def store(n, s):
                for j in range(2):
                    sp.wait_ge(s_y[j], n + 1)
                sp.dma_start(y_dram[n * BLOCK:n * BLOCK + BLOCK].rearrange("(p i) d -> p i d", i=NT)
                             if isinstance(n, int) else
                             y_dram[bass.ds(n * BLOCK, BLOCK)].rearrange("(p i) d -> p i d", i=NT),
                             yb[s][:, :, :]).then_inc(s_yb[s], 16)

            sp.wait_ge(s_tb, TB_N)
            load(0, 0)
            load(1, 1)

            def step(n, s):
                sp.wait_ge(s_wl, n * 3 + 3)
                sp.wait_ge(x_full, n * 2 + 2)
                load(n + 2, s)

            step(0, 0)
            FIRST = (n_batches - 4) // 2
            with sp.Fori(0, FIRST) as i:
                for u in range(2):
                    step(i * 2 + 1 + u, 1 - u)
                    store(i * 2 + u, u)
            sp.wait_ge(s_tail, experts * NT * 16)
            with sp.Fori(FIRST, PAIRS) as i:
                for u in range(2):
                    step(i * 2 + 1 + u, 1 - u)
                    store(i * 2 + u, u)
            for n in range(NBLK - 3, NBLK):
                store(n, n % 2)
            sp.wait_ge(s_yb[0], ((NBLK + 1) // 2) * 16)
            sp.wait_ge(s_yb[1], (NBLK // 2) * 16)

        @block.tensor
        def _(pe):
            pe.wait_ge(s_k, 8)
            pe.matmul(OB[0][:, 0:experts], fones[:, :], msum[:, :], start=True, stop=True).then_inc(s_cnt, 1)

            def turn(n, s, rows):
                pe.wait_ge(s_xb[s], rows)
                for k in range(KF):
                    pe.wait_ge(x_lo, n * 2 + k - 1 if not (isinstance(n, int) and n * 2 + k < 1) else 0)
                    for i in range(NT):
                        last = pe.transpose(TB[k][:, P * i:P * i + P], xb[s][:, i, P * k:P * k + P], fident[:, :])
                    last.then_inc(x_full, 1)

            def split(out, lh, ll, rh, rl, first, last):
                pe.matmul(out, lh, rh, start=first, stop=False)
                pe.matmul(out, lh, rl, start=False, stop=False)
                return pe.matmul(out, ll, rh, start=False, stop=last)

            def gate_up(n, s, m):
                if m == 0:
                    pe.wait_ge(x_lo, n * 2 + 2)
                    pe.wait_ge(s_wl, n * 3 + 2)
                k0 = n * MT + m
                for w, (bank, free, full) in enumerate([(GB, s_sg, g_full), (UB, s_am, u_full)]):
                    if not (isinstance(k0, int) and k0 < 1):
                        pe.wait_ge(free, k0 - 1)
                    for k in range(KF):
                        c = CH * w + inter * k + P * m
                        last = split(bank[m % 2][:, :], wh[s][:, c:c + P], wl[s][:, c:c + P],
                                     xh[s][:, k, :], xl[s][:, k, :], k == 0, k == KF - 1)
                    last.then_inc(full, 1)

            def down(n, s):
                pe.wait_ge(s_wl, n * 3 + 3)
                pe.wait_ge(s_al, n * MT + MT)
                for j in range(2):
                    pe.wait_ge(s_y[j], n)
                    for ii in range(2):
                        i = 2 * j + ii
                        for m in range(MT):
                            c = 2 * CH + D * m
                            last = split(OB[j][:, D * ii:D * ii + D], ah[s][:, m, P * i:P * i + P],
                                         al[s][:, m, P * i:P * i + P], wh[s][:, c:c + D], wl[s][:, c:c + D],
                                         m == 0, m == MT - 1)
                    last.then_inc(y_full, 1)

            turn(0, 0, 16)

            def body(n, s):
                gate_up(n, s, 0)
                gate_up(n, s, 1)
                if not isinstance(n, int) or n > 0:
                    down(n - 1, 1 - s)
                gate_up(n, s, 2)
                if not isinstance(n, int) or n < NBLK - 1:
                    turn(n + 1, 1 - s, (n + s) * 8 + 16)
                gate_up(n, s, 3)

            blocks(pe, body)
            down(NBLK - 1, 0)

        @block.scalar
        def _(act):
            def high(n, s):
                for k in range(KF):
                    act.wait_ge(x_full, n * 2 + k + 1)
                    act.activation(xh[s][:, k, :], TB[k][:, :], ACT.Copy).then_inc(x_hi, 1)

            def out(n, s, stored):
                act.wait_ge(s_yb[s], stored)
                for j in range(2):
                    act.wait_ge(y_full, n * 2 + j + 1)
                    act.activation(yb[s][:, 2 * j:2 * j + 2, :], OB[j][:, :].rearrange("p (i d) -> p i d", d=D),
                                   ACT.Copy).then_inc(s_y[j], 1)

            def silu(n, s, m):
                k0 = n * MT + m
                act.wait_ge(g_full, k0 + 1)
                if not (isinstance(k0, int) and k0 < 2):
                    act.wait_ge(s_am, k0 - 1)
                act.activation(sg[m % 2][:, :], GB[m % 2][:, :], ACT.Silu).then_inc(s_sg, 1)
                act.wait_ge(s_am, k0 + 1)
                act.activation(ah[s][:, m, :], am[m % 2][:, :], ACT.Copy).then_inc(s_ah, 1)

            high(0, 0)

            def body(n, s):
                silu(n, s, 0)
                silu(n, s, 1)
                if not isinstance(n, int) or n > 0:
                    out(n - 1, 1 - s, (n - 1 - (1 - s)) * 8)
                silu(n, s, 2)
                if not isinstance(n, int) or n < NBLK - 1:
                    high(n + 1, 1 - s)
                silu(n, s, 3)

            blocks(act, body)
            out(NBLK - 1, 0, (NBLK - 1) * 8)

        @block.vector
        def _(dve):
            step = [0]

            def chain(ins):
                step[0] += 1
                ins.then_inc(s_tb, 1)
                dve.wait_ge(s_tb, step[0])

            def over(a, shape, pattern):
                return a.rearrange(pattern, o=1).to_broadcast(shape)

            dve.wait_ge(s_k, 8)
            dve.tensor_copy(kf_[:, :], ki[:, :]).then_inc(s_k, 1)
            dve.tensor_copy(ef[:, :], ei[:, :]).then_inc(s_k, 1)
            dve.tensor_copy(jf[:, :], ji[:, :]).then_inc(s_k, 1)
            dve.tensor_copy(tofff[:, :, :], toff[:, :, :]).then_inc(s_k, 1)
            dve.memset(one9[:, :], 1.0).then_inc(s_k, 1)
            dve.memset(nblk[:, :], float(n_batches)).then_inc(s_k, 1)
            dve.wait_ge(s_k, 14)
            dve.tensor_scalar(est[:, :], ef[:, :], float(region), None, ALU.mult).then_inc(s_k, 1)
            dve.tensor_scalar(jr[:, :], jf[:, :], float(BLOCK), None, ALU.mult).then_inc(s_k, 1)
            dve.wait_ge(s_k, 16)
            dve.wait_ge(s_cnt, 1)
            chain(dve.tensor_copy(cnt[:, :], OB[0][:, 0:experts]))
            chain(dve.tensor_tensor(cmp[:, :, :], over(cnt[:, :], [P, experts, MAXB], "p (e o) -> p e o"),
                                    over(kf_[:, :], [P, experts, MAXB], "p (o k) -> p o k"), ALU.is_gt))
            chain(dve.tensor_reduce(nblk[:, 0:experts], cmp[:, :, :], AX_X, ALU.add))
            chain(dve.tensor_tensor_scan(cum[:, 0:experts], one9[:, 0:experts], nblk[:, 0:experts],
                                         float(n_batches), ALU.mult, ALU.add))
            chain(dve.tensor_copy(cum[:, experts:NE], nblk[:, experts:NE]))
            chain(dve.tensor_tensor(base[:, :], cum[:, :], nblk[:, :], ALU.subtract))
            chain(dve.scalar_tensor_tensor(out=shift[:, :], in0=base[:, :], scalar=float(BLOCK), in1=est[:, :],
                                           op0=ALU.mult, op1=ALU.subtract))
            jb = over(jf[:, :], [P, NBLK, NE], "p (j o) -> p j o")
            chain(dve.tensor_tensor(ge0[:, :, :], jb, over(base[:, :], [P, NBLK, NE], "p (o e) -> p o e"), ALU.is_ge))
            chain(dve.tensor_tensor(ge1[:, :, :], jb, over(cum[:, :], [P, NBLK, NE], "p (o e) -> p o e"), ALU.is_ge))
            chain(dve.tensor_tensor(ge0[:, :, :], ge0[:, :, :], ge1[:, :, :], ALU.subtract))
            chain(dve.tensor_tensor(rows[:, :, :], over(jr[:, :], [P, NBLK, NE], "p (j o) -> p j o"),
                                    over(shift[:, :], [P, NBLK, NE], "p (o e) -> p o e"), ALU.subtract))
            dve.tensor_tensor(rows[:, :, :], rows[:, :, :], ge0[:, :, :], ALU.mult).then_inc(s_k, 1)
            dve.tensor_tensor(ge1[:, :, :], ge0[:, :, :], over(ef[:, :], [P, NBLK, NE], "p (o e) -> p o e"),
                              ALU.mult).then_inc(s_k, 1)
            dve.tensor_tensor(tstart[:, :], cnt[:, :], est[:, 0:experts], ALU.add).then_inc(s_k, 1)
            dve.wait_ge(s_k, 19)
            dve.tensor_reduce(trf[:, :], rows[:, :, :], AX_X, ALU.add).then_inc(s_k, 1)
            dve.tensor_reduce(tef[:, :], ge1[:, :, :], AX_X, ALU.add).then_inc(s_k, 1)
            dve.tensor_tensor(tofff[:, :, :], tofff[:, :, :], over(tstart[:, :], [P, experts, NT], "p (e o) -> p e o"),
                              ALU.add).then_inc(s_k, 1)
            dve.wait_ge(s_k, 22)
            chain(dve.tensor_copy(tab_r[:, :], trf[:, :]))
            chain(dve.tensor_copy(tab_e[:, :], tef[:, :]))
            chain(dve.tensor_copy(tidx[:, :, :], tofff[:, :, :]))
            chain(dve.memset(shs[:, :], 0.0))
            assert step[0] == TB_N

            def high(n, s, part, landed):
                if part == 0:
                    dve.wait_ge(s_raw[s], landed)
                if part < 2:
                    dve.wait_ge(u_full, (n - 1) * MT if not (isinstance(n, int) and n < 1) else 0)
                else:
                    dve.wait_ge(y_full, (n - 1) * 2 if not (isinstance(n, int) and n < 1) else 0)
                c = slice(CH * part, CH * part + CH)
                dve.tensor_copy(wh[s][:, c], raw[s][:, c]).then_inc(s_wh, 1)

            def low_x(n, s):
                for k in range(KF):
                    dve.wait_ge(x_hi, n * 2 + k + 1)
                    dve.tensor_tensor(xl[s][:, k, :], TB[k][:, :], f32(xh[s][:, k, :]), ALU.subtract).then_inc(x_lo, 1)

            def mul(n, s, m):
                k0 = n * MT + m
                dve.wait_ge(u_full, k0 + 1)
                dve.wait_ge(s_sg, k0 + 1)
                if not (isinstance(k0, int) and k0 < 2):
                    dve.wait_ge(s_al, k0 - 1)
                dve.tensor_tensor(am[m % 2][:, :], sg[m % 2][:, :], UB[m % 2][:, :], ALU.mult).then_inc(s_am, 1)
                dve.wait_ge(s_ah, k0 + 1)
                dve.tensor_tensor(al[s][:, m, :], am[m % 2][:, :], f32(ah[s][:, m, :]), ALU.subtract).then_inc(s_al, 1)

            for part in range(3):
                high(0, 0, part, 16)
            low_x(0, 0)

            q = 4 * 2 * NT
            ohf = onehot[:, :, :, :].rearrange("p b j e -> p (b j) e")
            for c in range(n_batches * 2 * NT // q):
                dve.tensor_tensor(shf[:, :, :], ohf[:, q * c:q * c + q, :],
                                  over(shift[:, 0:experts], [P, q, experts], "p (o e) -> p o e"),
                                  ALU.mult).then_inc(s_fx, 1)
                dve.wait_ge(s_fx, 2 * c + 1)
                dve.tensor_reduce(shs[:, q * c:q * c + q], shf[:, :, :], AX_X, ALU.add).then_inc(s_fx, 1)
                dve.wait_ge(s_fx, 2 * c + 2)
            dve.tensor_tensor(shs[:, :], shs[:, :], slot[:, :, :].rearrange("p b j -> p (b j)"),
                              ALU.add).then_inc(s_fx, 1)
            dve.wait_ge(s_fx, n_batches * 2 * NT // q * 2 + 1)
            dve.tensor_copy(fidx[:, :, :].rearrange("p b j -> p (b j)"), shs[:, :]).then_inc(s_fx, 1)

            def body(n, s):
                more = not isinstance(n, int) or n < NBLK - 1
                landed = (n + s) * 8 + 16
                if more:
                    high(n + 1, 1 - s, 0, landed)
                    high(n + 1, 1 - s, 1, landed)
                mul(n, s, 0)
                mul(n, s, 1)
                if more:
                    high(n + 1, 1 - s, 2, landed)
                mul(n, s, 2)
                if more:
                    low_x(n + 1, 1 - s)
                mul(n, s, 3)

            blocks(dve, body)


def f32(t):
    return t.bitcast(F32)


def combine_phase(nc, sems, x1_dram, y_dram, out, fidx, weight, nb):
    D = out.shape[2]
    NT = out.shape[1] // P
    ctx = ExitStack()
    with ctx:
        def sb(name, shape, dt=F32):
            return ctx.enter_context(nc.sbuf_tensor(name, shape, dt))

        def sem(name):
            return sems.enter_context(nc.semaphore(name))

        xa = [sb(f"cxa{s}", [P, NT, D]) for s in range(2)]
        ya = [sb(f"cya{s}", [P, NT, D]) for s in range(2)]
        yr = [sb(f"cyr{s}", [P, 2 * NT, D]) for s in range(2)]
        ob = [sb(f"cob{s}", [P, NT, D]) for s in range(2)]
        si = [sb(f"csi{s}", [P, 2 * NT], U32) for s in range(2)]
        sw = [sb(f"csw{s}", [P, 2 * NT]) for s in range(2)]
        s_in = [sem(f"c_in{s}") for s in range(2)]
        s_gat = [sem(f"c_gat{s}") for s in range(2)]
        s_out = [sem(f"c_out{s}") for s in range(2)]
        s_ix = sem("c_ix")
        s_add = sem("c_add")

        s_held_dve, s_held_pool = sem("c_held_dve"), sem("c_held_pool")
        PER = 1 + 2 * NT

        block = ctx.enter_context(nc.Block())
        x1_t = x1_dram.rearrange("(b i p) d -> b p i d", p=P, i=NT)
        ys_t = y_dram[0:nb * NT * P].rearrange("(b i p) d -> b p i d", p=P, i=NT)
        out_t = out.rearrange("b (i p) d -> b p i d", p=P)

        def pairs(eng, body):
            body(0)
            with eng.Fori(1, nb // 2) as i:
                body(i)

        def at(t, b):
            return t[bass.ds(b, 1)].rearrange("o p i d -> p (o i) d")

        @block.sync
        def _(sp):
            def body(i):
                for s in range(2):
                    b = i * 2 + s
                    sp.wait_ge(s_add, i * 2 * PER)
                    sp.dma_start(xa[s][:, :, :], at(x1_t, b)).then_inc(s_in[s], 16)
                    sp.dma_start(ya[s][:, :, :], at(ys_t, b)).then_inc(s_in[s], 16)
                for s in range(2):
                    b = i * 2 + s
                    sp.wait_ge(s_add, b * PER + PER)
                    sp.dma_start(at(out_t, b), ob[s][:, :, :]).then_inc(s_out[s], 16)

            pairs(sp, body)
            for s in range(2):
                sp.wait_ge(s_out[s], nb // 2 * 16)

        @block.gpsimd
        def _(pool):
            def body(i):
                for s in range(2):
                    b = i * 2 + s
                    pool.wait_ge(s_ix, b * 2 + 2)
                    pool.nop().then_inc(s_held_pool, 1)
                    for j in range(2 * NT):
                        pool.indirect_dma_start(
                            out=yr[s][:, j, :], out_offset=None, in_=y_dram,
                            in_offset=bass.IndirectOffsetOnAxis(ap=si[s][:, j:j + 1], axis=0)
                        ).then_inc(s_gat[s], 16)

            pairs(pool, body)

        @block.vector
        def _(dve):
            def places(b, s):
                dve.nop().then_inc(s_held_dve, 1)
                dve.tensor_copy(si[s][:, :], fidx[:, bass.ds(b, 1), :].rearrange("p o j -> p (o j)")
                                ).then_inc(s_ix, 1)
                dve.tensor_copy(sw[s][:, :], weight[:, bass.ds(b, 1), :].rearrange("p o j -> p (o j)")
                                ).then_inc(s_ix, 1)

            def total(b, s, i):
                dve.wait_ge(s_in[s], i * 32 + 32)
                dve.wait_ge(s_out[s], i * 16)
                dve.tensor_tensor(ob[s][:, :, :], xa[s][:, :, :], ya[s][:, :, :], ALU.add).then_inc(s_add, 1)
                dve.wait_ge(s_gat[s], i * 2 * NT * 16 + 2 * NT * 16)
                dve.wait_ge(s_ix, b * 2 + 2)
                for k in range(2):
                    dve.wait_ge(s_add, b * PER + 1 + k * NT)
                    for t in range(NT):
                        j = 2 * t + k
                        dve.scalar_tensor_tensor(out=ob[s][:, t, :], in0=yr[s][:, j, :], scalar=sw[s][:, j:j + 1],
                                                 in1=ob[s][:, t, :], op0=ALU.mult, op1=ALU.add).then_inc(s_add, 1)

            def body(i):
                for s in range(2):
                    if s == 0:
                        dve.wait_ge(s_add, i * 2 * PER)
                        places(i * 2, 0)
                        places(i * 2 + 1, 1)
                    total(i * 2 + s, s, i)

            pairs(dve, body)


def program(nc, x, adj, wqkv, wgate, bg, router_w, w_all, out):
    nb, n, d = x.shape
    experts = router_w.shape[1]
    inter = w_all.shape[2] * P // (3 * d)
    tokens = nb * n
    routed = (2 * tokens + experts * (BLOCK - 1)) // BLOCK
    region = tokens + BLOCK
    nt = n // P
    xn_dram = nc.dram_tensor("xn_dram", (tokens, d), F32, kind="Internal").ap()
    x1_dram = nc.dram_tensor("x1_dram", (tokens, d), F32, kind="Internal").ap()
    xg_dram = nc.dram_tensor("xg_dram", (experts * region + tokens, d), F32, kind="Internal").ap()
    y_dram = nc.dram_tensor("y_dram", ((nb + routed) * BLOCK, d), F32, kind="Internal").ap()
    xs_dram = xg_dram[experts * region:experts * region + tokens]

    with ExitStack() as ctx:
        def sb(name, shape, dt=F32):
            return ctx.enter_context(nc.sbuf_tensor(name, shape, dt))

        onehot = sb("onehot", [P, nb, 2 * nt, experts], BF16)
        slot = sb("slot", [P, nb, 2 * nt])
        weight = sb("weight", [P, nb, 2 * nt])
        msum = sb("msum", [P, experts], BF16)
        fidx = sb("fidx", [P, nb, 2 * nt], U32)
        attention_phase(nc, ctx, x, adj, wqkv, wgate, bg, router_w, xn_dram, x1_dram, xs_dram, xg_dram,
                        onehot, slot, weight, msum, region)
        ffn_phase(nc, ctx, w_all, xg_dram, y_dram, onehot, slot, msum, fidx, nb, region, experts, inter)
        combine_phase(nc, ctx, x1_dram, y_dram, out, fidx, weight, nb)


def kernel(x, adj, L0_gnn_Wq, L0_gnn_Wk, L0_gnn_Wv, L0_gnn_Wg, L0_gnn_bg, L0_ffn_router_w,
           L0_ffn_Wg, L0_ffn_Wu, L0_ffn_Wd, L0_ffn_Sg, L0_ffn_Su, L0_ffn_Sd):
    import numpy as np
    import concourse.bacc as bacc
    from concourse.bass_utils import run_bass_kernel_spmd

    def rows(w):
        w = np.asarray(w)
        e, k, n = w.shape
        return w.reshape(e, k // P, P, n).transpose(0, 2, 1, 3).reshape(e, P, k // P * n)

    arrays = {
        "x": np.asarray(x),
        "adj": np.asarray(adj),
        "wqkv": np.concatenate([np.asarray(w).T for w in (L0_gnn_Wq, L0_gnn_Wk, L0_gnn_Wv)], axis=1),
        "wgate": np.asarray(L0_gnn_Wg).T,
        "bg": np.asarray(L0_gnn_bg),
        "router_w": np.asarray(L0_ffn_router_w),
        "w_all": np.concatenate([np.concatenate([rows(w), rows(np.asarray(s)[None])], axis=0) for w, s in (
            (L0_ffn_Wg, L0_ffn_Sg), (L0_ffn_Wu, L0_ffn_Su), (L0_ffn_Wd, L0_ffn_Sd))], axis=2),
    }
    nc = bacc.Bacc("TRN2", target_bir_lowering=False, num_devices=1)
    in_map, args = {}, []
    for name, a in arrays.items():
        a = np.ascontiguousarray(a)
        in_map[f"in_{name}"] = a
        args.append(nc.dram_tensor(f"in_{name}", a.shape, mybir.dt.from_np(a.dtype), kind="ExternalInput").ap())
    out = nc.dram_tensor("out_x", tuple(arrays["x"].shape), F32, kind="ExternalOutput").ap()
    program(nc, *args, out)
    r = run_bass_kernel_spmd(nc, [in_map], core_ids=[0])
    return r.results[0]["out_x"]
```

```python
from contextlib import ExitStack

import concourse.bass as bass
from concourse import mybir

P = 128
F32 = mybir.dt.float32
F32R = mybir.dt.float32r
BF16 = mybir.dt.bfloat16
I32 = mybir.dt.int32
U32 = mybir.dt.uint32
ALU = mybir.AluOpType
ACT = mybir.ActivationFunctionType
AX_X = mybir.AxisListType.X

LN_EPS = 1e-5
MASKED = -1e30
BLOCK = 512
XW = 256 + 4


UNIT_AT = {"R0": 2, "G0": 4, "G1": 6, "C0": 8, "C1": 9, "P0": 10, "P1": 11, "Z0": 12, "Z1": 13, "Q0": 14,
           "K0": 15, "V0": 17, "V1": 18, "Q1": 19, "K1": 20, "M0": 22, "M1": 23, "X0": 24, "X1": 25,
           "L0": 27, "T0": 28}
ACT_AT = {"exp": 0, "tanh": 14}
DVE_AT = {"mark": 0, "weigh": 2, "place": 3, "stat": 4, "var": 5, "norm1": 6, "xn0": 8, "xn1": 9,
          "bias0": 11, "bias1": 14, "gate": 17, "x1": 18, "stat2": 19, "var2": 20, "xn2": 22, "norm0": 24,
          "choose": 30}
POOL_AT = {"scatter": 3, "rstd": 6, "diff": 11, "x1": 14, "rstd2": 20}
HIGH_ON_DVE = {0, 1, 8, 9, 10, 20, 21, 24, 25, 27, 28, 29}


def attention_phase(nc, sems, x, adj, wqkv, wgate, bg, router_w, xn_dram, x1_dram, xt2_dram, xg_dram,
                    ident, msum, xn2, idx, s_scat, region):
    NB, N, D = x.shape
    NT = N // P
    NH = 8
    DK = D // NH
    KF = D // P
    HPT = P // DK
    SCALE = float(DK) ** -0.5
    E = router_w.shape[1]
    AHEAD = 2
    LAG = 3
    POS = NH * NT
    VW = 2 * DK + 2

    ctx = ExitStack()
    with ctx:
        def sb(name, shape, dt=F32):
            return ctx.enter_context(nc.sbuf_tensor(name, shape, dt))

        def sem(name):
            return sems.enter_context(nc.semaphore(name))

        banks = [ctx.enter_context(nc.psum_tensor(f"bank{i}", [P, 512], F32)) for i in range(8)]
        S = banks[0:2]
        T = banks[2:4]
        C = banks[4]
        BT = banks[5]
        G = banks[6:8]

        xn = sb("xn", [P, NT, D])
        xp = sb("xp", [P, NT, D])
        xnp = sb("xnp", [P, NT, D])
        adj_i = sb("adj_i", [P, 2, N], I32)
        bias_q = [sb(f"bias_q{s}", [P, NT, N], BF16) for s in range(2)]
        bias_t = [sb(f"bias_t{s}", [P, NT, N], BF16) for s in range(2)]
        xt_h = sb("xt_h", [P, KF, N], F32R)
        xt_l = sb("xt_l", [P, KF, N], F32R)
        gx = [sb(f"gx{s}", [P, NT, D]) for s in range(2)]
        QH, QL, KH, KL = range(4)
        qk = sb("qk", [P, KF, 4, N], F32R)
        stack = sb("stack", [P, NH, 2, N], F32R)
        SR = 3 * DK
        v = [sb(f"v{s}", [P, NT, NH, VW], F32R) for s in range(2)]
        pf = [sb(f"pf{i}", [P, N]) for i in range(4)]
        ph = [sb(f"ph{i}", [P, N], F32R) for i in range(4)]
        pl = [sb(f"pl{i}", [P, N], F32R) for i in range(4)]
        ct = [sb(f"ct{i}", [P, N]) for i in range(2)]
        cb = sb("cb", [P, NH, NT, VW])
        rden = sb("rden", [P, NH, NT])
        c_tok = sb("c_tok", [P, NT, D])
        ct_h = sb("ct_h", [P, KF, N], F32R)
        ct_l = sb("ct_l", [P, KF, N], F32R)
        z = sb("z", [P, NT, D])
        diff = sb("diff", [P, NT, D])
        x1 = sb("x1", [P, NT, D])
        W0, W1, WE, WT = D, D + 1, D + 2, D + 3
        wqkv_h = sb("wqkv_h", [P, KF, 3 * D], F32R)
        wqkv_l = sb("wqkv_l", [P, KF, 3 * D], F32R)
        wg_h = sb("wg_h", [P, 2 * KF, D], F32R)
        wg_l = sb("wg_l", [P, 2 * KF, D], F32R)
        bgt = sb("bgt", [P, D])
        rw = sb("rw", [P, KF, E])
        ident_b = sb("ident_b", [P, P], BF16)
        below = sb("below", [P, P], BF16)
        ones_b = sb("ones_b", [P, P], BF16)
        iota_i = sb("iota_i", [P, E], I32)
        iota_e = sb("iota_e", [P, E])
        tok_i = sb("tok_i", [P, NT], I32)
        onehot = sb("onehot", [P, 2 * NT, E], BF16)
        slot = sb("slot", [P, 2 * NT])
        start_e = sb("start_e", [P, E])
        stats = sb("stats", [P, NT, 6])
        stats2 = sb("stats2", [P, NT, 6])
        mv = sb("mv", [P, NT, 2])
        mv2 = sb("mv2", [P, NT, 2])
        vr = sb("vr", [P, NT])
        vr2 = sb("vr2", [P, NT])
        rstd = sb("rstd", [P, NT])
        rstd2 = sb("rstd2", [P, NT])
        mhalf = sb("mhalf", [P, NT])
        mx = sb("mx", [P, 2, NT])
        mcol = sb("mcol", [P, 2, 2, NT])
        row = sb("row", [2 * NT, 4, P], F32R)
        lg = sb("lg", [P, NT, E])
        mx8 = sb("mx8", [P, NT, 8])
        ix8 = sb("ix8", [P, NT, 8], U32)
        ef = sb("ef", [P, NT, 2])
        mb = sb("mb", [P, NT, E], BF16)
        msd = sb("msd", [P, E])
        posb = sb("posb", [P, NT, E])
        pick = sb("pick", [P, NT, 2, E])
        dl = sb("dl", [P, NT])
        el = sb("el", [P, NT])
        ea = sb("ea", [P, NT])

        s_w = sem("s_w")
        s_const = sem("s_const")
        s_set = sem("s_set")
        s_x = sem("s_x")
        s_adj = sem("s_adj")
        s_bias = sem("s_bias")
        s_stat = sem("s_stat")
        s_rstd = sem("s_rstd")
        s_xn = sem("s_xn")
        s_xnst = sem("s_xnst")
        s_xp = sem("s_xp")
        g_full = sem("g_full")
        g_hi = sem("g_hi")
        g_free = sem("g_free")
        s_ref = [sem(f"s_ref{h}") for h in range(NH)]
        s_row = [sem(f"s_row{h}") for h in range(NH)]
        s_full = sem("s_full")
        s_done = sem("s_done")
        s_mcol = sem("s_mcol")
        t_full = sem("t_full")
        p_exp = sem("p_exp")
        p_hi = sem("p_hi")
        p_lo = sem("p_lo")
        pv = sem("pv")
        s_ct = sem("s_ct")
        b_full = sem("b_full")
        b_free = sem("b_free")
        s_norm = sem("s_norm")
        s_z = sem("s_z")
        s_d = sem("s_d")
        s_mix = sem("s_mix")
        s_stat2 = sem("s_stat2")
        s_rstd2 = sem("s_rstd2")
        s_xn2 = sem("s_xn2")
        s_st = sem("s_st")
        s_rt = sem("s_rt")
        s_el = sem("s_el")
        s_rt0 = sem("s_rt0")
        s_lo = sem("s_lo")
        s_half = sem("s_half")

        s_held_pe, s_held_dve, s_held_pool, s_held_sp = (sem(f"s_held_{e}") for e in ("pe", "dve", "pool", "sp"))

        RT_MAX = NT
        RT_IX = RT_MAX + NT
        RT_EF = RT_IX + 1
        RT_OH = RT_EF + 1
        RT_MB = RT_OH + 1
        RT_DL = RT_MB + 1
        RT_MSD = RT_DL + 1
        RT_EA = RT_MSD + 1
        RT_W0 = RT_EA + 1
        RT_W1 = RT_W0 + 3
        RT_MS = RT_W1 + 1
        RT_PICK = RT_MS + 1
        RT_SLOT = RT_PICK + 1
        RT_IDX = RT_SLOT + 1
        RT = RT_IDX

        block = ctx.enter_context(nc.Block())

        x_t = x.rearrange("b (i p) d -> b p i d", p=P)
        adj_t = adj.rearrange("b (i p) n -> b p i n", p=P)
        xn_t = xn_dram.rearrange("(b i p) d -> b p i d", p=P, i=NT)
        x1_t = x1_dram.rearrange("(b i p) d -> b p i d", p=P, i=NT)

        UNITS = {p: name for name, p in sorted(UNIT_AT.items(), key=lambda x: x[1])}
        ORDER = list(UNITS.values())
        NU = len(ORDER)
        HI = [u for u in ORDER if u[0] in "PQKVC"]

        def has(b, name, att, pre, post):
            kind = name[0]
            return late(b) if kind == "R" else att if kind == "G" else post if kind in "CZXLT" else pre

        def late(b):
            return b >= 2 if isinstance(b, int) else True

        def unit(b, name):
            return (b + 1) * NU + ORDER.index(name)

        def bank(par, name):
            return G[(par * NU + ORDER.index(name)) % 2]

        def hi_index(b, name):
            return (b + 1) * len(HI) + HI.index(name)

        def iterations(eng, body):
            body(-1, 0, False, True, False)
            body(0, 1, True, True, False)
            body(1, 0, True, True, True)
            body(2, 1, True, True, True)
            with eng.Fori(1, (NB - 2) // 2) as i:
                body(i * 2 + 1, 0, True, True, True)
                body(i * 2 + 2, 1, True, True, True)
            body(NB - 1, 0, True, False, True)
            body(NB, 1, False, False, True)

        def ahead(b, h, att, pre):
            return (b, h + AHEAD, att) if h + AHEAD < NH else (b + 1, h + AHEAD - NH, pre)

        def behind(b, p, lag, att):
            if p >= lag:
                return b, p - lag, att
            before = att if not isinstance(b, int) else 0 < b <= NB
            return b - 1, p - lag + POS, before

        def f32(t):
            return t.bitcast(F32)

        @block.sync
        def _(sp):
            sp.dma_start(xn[:, :, :], x_t[0]).then_inc(s_x, 16)
            sp.dma_start(z[:, 0:3, :].rearrange("p i d -> p (i d)").rearrange("p (k n) -> p k n", k=1),
                         wqkv[0:P, :].rearrange("(k p) n -> p k n", p=P)).then_inc(s_w, 16)
            sp.dma_start(diff[:, 0:3, :].rearrange("p i d -> p (i d)").rearrange("p (k n) -> p k n", k=1),
                         wqkv[P:2 * P, :].rearrange("(k p) n -> p k n", p=P)).then_inc(s_w, 16)
            sp.dma_start(x1[:, :, :], wgate.rearrange("(k p) n -> p k n", p=P)).then_inc(s_w, 16)
            sp.dma_start(rw[:, :, :], router_w.rearrange("(k p) e -> p k e", p=P)).then_inc(s_w, 16)
            sp.dma_start(bgt[:, :], bg.rearrange("(o d) -> o d", o=1).to_broadcast([P, D])).then_inc(s_w, 16)

            def body(b, par, att, pre, post):
                B = b + 1
                A = b - 1
                if pre:
                    if not isinstance(B, int) or B > 0:
                        sp.wait_ge(g_full, unit(b - 1, "P1") + 1)
                        sp.wait_ge(s_xnst, B * 16)
                        sp.dma_start(xn[:, :, :], x_t[bass.ds(B, 1)].rearrange("o p i d -> p (o i) d")
                                     if not isinstance(B, int) else x_t[B]).then_inc(s_x, 16)
                    sp.wait_ge(s_bias, B * 2)
                    sp.dma_start(adj_i[:, :, :], (adj_t[B] if isinstance(B, int) else
                                 adj_t[bass.ds(B, 1)].rearrange("o p i n -> p (o i) n"))[:, 0:2]).then_inc(s_adj, 16)
                if post:
                    sp.wait_ge(s_d, A * 2)
                    sp.wait_ge(s_xnst, A * 16 + 16)
                    dyn = not isinstance(A, int)
                    sp.dma_start(xp[:, :, :], x_t[bass.ds(A, 1)].rearrange("o p i d -> p (o i) d")
                                 if dyn else x_t[A]).then_inc(s_xp, 16)
                    sp.dma_start(xnp[:, :, :], xn_t[bass.ds(A, 1)].rearrange("o p i d -> p (o i) d")
                                 if dyn else xn_t[A]).then_inc(s_xp, 16)
                for h in range(NH):
                    if h == 2 and pre:
                        sp.wait_ge(s_xn, B * NT + NT)
                        sp.dma_start(xn_t[B] if isinstance(B, int) else
                                     xn_t[bass.ds(B, 1)].rearrange("o p i d -> p (o i) d"),
                                     xn[:, :, :]).then_inc(s_xnst, 16)
                    if h == 3 and pre:
                        sp.wait_ge(s_bias, B * 2 + 1)
                        sp.dma_start(adj_i[:, :, :], (adj_t[B] if isinstance(B, int) else
                                     adj_t[bass.ds(B, 1)].rearrange("o p i n -> p (o i) n"))[:, 2:4]).then_inc(s_adj, 16)
                    gb, gh, there = ahead(b, h, att, pre)
                    if there:
                        sp.wait_ge(s_done, (gb * NH + gh) * (NT + 1) + NT + 1)
                        sp.dma_start(f32(stack[SR:SR + 2, gh, 0, :]).rearrange("t (i c) -> t i c", c=P),
                                     f32(row[:, gh % 4, :])).then_inc(s_row[gh], 16)
                    for r in {4: [0, 1], 5: [2, 3], 6: [4, 5], 7: [6, 7]}.get(h, []):
                        if not pre:
                            continue
                        if att:
                            sp.wait_ge(t_full, b * POS + r * NT + NT)
                            sp.nop().then_inc(s_held_sp, 1)
                        m, j = r // HPT, r % HPT
                        sp.wait_ge(g_free, unit(b, "K0" if m == 0 else "K1") + 1)
                        for rows, (a, c) in enumerate([(QH, KH), (QL, KH), (QH, KL)]):
                            sp.dma_start(f32(stack[DK * rows:DK * rows + DK, r, :, :]),
                                         f32(qk[DK * j:DK * j + DK, m, a:c + 1:c - a, :])).then_inc(s_ref[r], 16)
                    dyn = not isinstance(A, int)
                    if h == 6 and post:
                        sp.wait_ge(s_mix, A * 2 + 2)
                        sp.dma_start(x1_t[bass.ds(A, 1)].rearrange("o p i d -> p (o i) d")
                                     if dyn else x1_t[A], x1[:, :, :]).then_inc(s_st, 16)
                    if h == 7 and post:
                        sp.wait_ge(g_free, unit(b, "X1") + 1)
                        sp.dma_start(xt2_dram[bass.ds(A, 1)].rearrange("o p c -> p (o c)")
                                     if dyn else xt2_dram[A],
                                     z[:, :, :].rearrange("p i d -> p (i d)")).then_inc(s_st, 16)

            iterations(sp, body)
            sp.wait_ge(s_st, NB * 32)

        @block.tensor
        def _(pe):
            pe.wait_ge(s_const, 9)

            def split(out, lh, ll, rh, rl, first, last):
                pe.matmul(out, lh, rh, start=first, stop=False)
                pe.matmul(out, lh, rl, start=False, stop=False)
                return pe.matmul(out, ll, rh, start=False, stop=last)

            def turn(out, src, kf):
                for i in range(NT):
                    last = pe.transpose(out[:, P * i:P * i + P], src[:, i, P * kf:P * kf + P], ident[:, :])
                return last

            def do_unit(b, par, name):
                B, A = b + 1, b - 1
                o = bank(par, name)
                k = int(name[1])
                s = par
                if not (isinstance(b, int) and b == -1 and ORDER.index(name) == 0):
                    pe.wait_ge(g_free, unit(b, name) - 1)
                if name[0] == "P":
                    pe.wait_ge(s_xn, B * NT + NT)
                    last = turn(o, xn, k)
                elif name[0] in "QK":
                    if isinstance(b, int) and b == -1:
                        pe.wait_ge(s_set, 14)
                    pe.wait_ge(g_free, unit(b, "P1") + 1)
                    c0 = (D if name[0] == "K" else 0) + P * k
                    for kf in range(KF):
                        last = split(o[:, :], wqkv_h[:, kf, c0:c0 + P], wqkv_l[:, kf, c0:c0 + P],
                                     xt_h[:, kf, :], xt_l[:, kf, :], kf == 0, kf == KF - 1)
                elif name[0] in "VG":
                    for ii in range(2):
                        i = 2 * k + ii
                        for kf in range(KF):
                            wh, wl = ((wqkv_h[:, kf, 2 * D:], wqkv_l[:, kf, 2 * D:]) if name[0] == "V" else
                                      (wg_h[:, KF + kf, :], wg_l[:, KF + kf, :]))
                            last = split(o[:, D * ii:D * ii + D], xt_h[:, kf, P * i:P * i + P],
                                         xt_l[:, kf, P * i:P * i + P], wh, wl, kf == 0, kf == KF - 1)
                elif name[0] == "M":
                    pe.wait_ge(s_bias, B * 2 + 2)
                    ob = o[:, :].bitcast(BF16)
                    for kk in range(2):
                        for i in range(NT):
                            kt = 2 * k + kk
                            last = pe.transpose(ob[:, N * kk + P * i:N * kk + P * i + P],
                                                bias_q[s][:, i, P * kt:P * kt + P], ident_b[:, :])
                elif name[0] == "C":
                    pe.wait_ge(s_norm, A * 6 + 6)
                    last = turn(o, c_tok, k)
                elif name[0] == "Z":
                    pe.wait_ge(g_free, unit(b, "C1") + 1)
                    for ii in range(2):
                        i = 2 * k + ii
                        for kf in range(KF):
                            last = split(o[:, D * ii:D * ii + D], ct_h[:, kf, P * i:P * i + P],
                                         ct_l[:, kf, P * i:P * i + P], wg_h[:, kf, :], wg_l[:, kf, :],
                                         kf == 0, kf == KF - 1)
                elif name[0] == "X":
                    pe.wait_ge(s_xn2, A * NT + NT)
                    last = turn(o, xn2, k)
                elif name[0] == "L":
                    pe.wait_ge(g_free, unit(b, "X1") + 1)
                    zt = z[:, :, :].rearrange("p i d -> p (i d)")
                    for kf in range(KF):
                        last = pe.matmul(o[0:E, :], rw[:, kf, :], zt[:, N * kf:N * kf + N],
                                         start=kf == 0, stop=kf == KF - 1)
                elif name[0] == "T":
                    pe.wait_ge(g_free, unit(b, "L0") + 1)
                    pe.nop().then_inc(s_held_pe, 1)
                    lgt = diff[:, :, :].rearrange("p i d -> p (i d)")
                    for i in range(NT):
                        last = pe.transpose(o[:, E * i:E * i + E], lgt[0:E, P * i:P * i + P], ident[0:E, 0:E])
                elif name[0] == "R":
                    pe.wait_ge(s_rt, (b - 2) * RT + RT_MB)
                    for i in range(NT):
                        pe.matmul(o[:, E * i:E * i + E], below[:, :], mb[:, i, :], start=True, stop=False)
                        for j in range(i):
                            pe.matmul(o[:, E * i:E * i + E], ones_b[:, :], mb[:, j, :], start=False, stop=False)
                        last = pe.matmul(o[:, E * i:E * i + E], ones_b[:, :], msum[:, :], start=False, stop=True)
                last.then_inc(g_full, 1)

            def body(b, par, att, pre, post):
                here = 1 - par
                for h in range(NH):
                    for t in range(NT):
                        p = h * NT + t
                        if att:
                            n = b * POS + p
                            if t == 0:
                                pe.wait_ge(s_row[h], b * 16 + 16)
                            if p == 0:
                                pe.wait_ge(g_free, unit(b - 1, "M1") + 1)
                            if not isinstance(b, int) or b > 0 or p >= 2:
                                pe.wait_ge(p_exp, n - 1)
                            o = T[p % 2]
                            pe.matmul(o[:, :], stack[0:SR + 2, h, 1, P * t:P * t + P], stack[0:SR + 2, h, 0, :],
                                      start=True, stop=False)
                            pe.matmul(o[:, :], ident_b[:, :], bias_t[here][:, t, :],
                                      start=False, stop=True).then_inc(t_full, 1)
                        gb, gh, there = ahead(b, h, att, pre)
                        if there:
                            g5 = (gb * NH + gh) * (NT + 1)
                            first = isinstance(gb, int) and gb == 0 and gh == 0
                            for i in {0: [0, 1], 1: [2, 3]}.get(t, []):
                                if i == 0:
                                    pe.wait_ge(s_ref[gh], gb * 48 + 48)
                                if not first or i >= 2:
                                    pe.wait_ge(s_done, g5 + i - 1)
                                pe.matmul(S[(gh * (NT + 1) + i) % 2][:, :], stack[0:SR, gh, 0, P * i:P * i + P],
                                          stack[0:SR, gh, 1, :], start=True, stop=True).then_inc(s_full, 1)
                        if p in UNITS:
                            name = UNITS[p]
                            if has(b, name, att, pre, post):
                                do_unit(b, par, name)
                            else:
                                pe.wait_ge(g_full, unit(b, name))
                                pe.nop().then_inc(g_full, 1)
                        eb, ep, was = behind(b, p, LAG, att)
                        if was:
                            eh, et = ep // NT, ep % NT
                            vs = v[here if ep <= p else par]
                            if ep == 0:
                                pe.wait_ge(g_free, unit(eb - 1, "V1") + 1)
                            if et == 0 and not (isinstance(eb, int) and eb == 0 and eh == 0):
                                pe.wait_ge(s_ct, eb * NH + eh)
                            pe.wait_ge(p_lo, eb * POS + ep + 1)
                            pe.matmul(C[0:2 * DK + 1, :], vs[:, et, eh, 0:2 * DK + 1], ph[ep % 4][:, :],
                                      start=et == 0, stop=False)
                            pe.matmul(C[0:2 * DK + 1, :], vs[:, et, eh, 0:2 * DK + 1], pl[ep % 4][:, :],
                                      start=False, stop=et == NT - 1).then_inc(pv, 1)
                        if there and t == NT - 1:
                            pe.wait_ge(s_mcol, (gb * NH + gh) * 2 + 2)
                            pe.wait_ge(s_done, g5 + NT - 1)
                            pe.transpose(S[(gh * (NT + 1) + NT) % 2][0:2 * NT, 0:P],
                                         mcol[:, gh % 2, :, :].rearrange("p t i -> p (t i)"),
                                         ident[:, :]).then_inc(s_full, 1)
                        eb, ep, was = behind(b, p, 2 * NT, att)
                        if was and t == 0:
                            eh = ep // NT
                            pe.wait_ge(s_ct, eb * NH + eh + 1)
                            pe.wait_ge(b_free, eb * NH + eh)
                            for i in range(NT):
                                last = pe.transpose(BT[:, VW * i:VW * i + 2 * DK + 1],
                                                    ct[eh % 2][0:2 * DK + 1, P * i:P * i + P],
                                                    ident[0:2 * DK + 1, 0:2 * DK + 1])
                            last.then_inc(b_full, 1)

            iterations(pe, body)
            do_unit(NB + 1, NB % 2, "R0")

        @block.scalar
        def _(act):
            act.wait_ge(s_w, 80)
            zf = z[:, :, :].rearrange("p i d -> p (i d)")
            df = diff[:, :, :].rearrange("p i d -> p (i d)")
            act.activation(wqkv_h[:, 0, :], zf[:, 0:3 * D], ACT.Copy).then_inc(s_set, 1)
            act.activation(wqkv_h[:, 1, :], df[:, 0:3 * D], ACT.Copy).then_inc(s_set, 1)
            act.activation(wg_h[:, :, :], x1[:, :, :], ACT.Copy).then_inc(s_set, 1)

            def evacuate(b, par, name):
                B, A = b + 1, b - 1
                o = bank(par, name)
                k = int(name[1])
                act.wait_ge(g_full, unit(b, name) + 1)
                if name[0] in "MXLT":
                    act.wait_ge(g_free, unit(b, name))
                if name[0] == "P":
                    act.activation(xt_h[:, k, :], o[:, :], ACT.Copy).then_inc(g_hi, 1)
                elif name[0] in "QK":
                    if name == "Q0":
                        for h in range(NH):
                            act.wait_ge(s_ref[h], B * 48)
                    act.activation(qk[:, k, QH if name[0] == "Q" else KH, :], o[:, :], ACT.Copy).then_inc(g_hi, 1)
                elif name[0] == "V":
                    if att_before(b):
                        act.wait_ge(pv, b * POS)
                    act.activation(v[par][:, 2 * k:2 * k + 2, :, 0:DK].rearrange("p i h d -> p (i h) d"),
                                   o[:, :].rearrange("p (j d) -> p j d", d=DK), ACT.Copy).then_inc(g_hi, 1)
                elif name[0] == "M":
                    if att_before(b):
                        act.wait_ge(t_full, b * POS)
                    act.activation(bias_t[par][:, 2 * k:2 * k + 2, :], o[:, :].bitcast(BF16).rearrange(
                        "p (i n) -> p i n", n=N), ACT.Copy).then_inc(g_free, 1)
                elif name[0] == "C":
                    act.activation(ct_h[:, k, :], o[:, :], ACT.Copy).then_inc(g_hi, 1)
                elif name[0] == "X":
                    act.wait_ge(s_mix, A * 2 + 1)
                    act.activation(zf[:, N * k:N * k + N], o[:, :], ACT.Copy).then_inc(g_free, 1)
                elif name[0] == "L":
                    act.wait_ge(s_mix, A * 2 + 2)
                    act.activation(df[0:E, 0:N], o[0:E, :], ACT.Copy).then_inc(g_free, 1)
                elif name[0] == "T":
                    act.wait_ge(s_rt, A * RT)
                    act.activation(lg[:, :, :], o[:, 0:NT * E].rearrange("p (i e) -> p i e", e=E),
                                   ACT.Copy).then_inc(g_free, 1)

            def second_choice(A):
                act.wait_ge(s_rt, A * RT + RT_DL)
                act.activation(el[:, :], dl[:, :], ACT.Exp).then_inc(s_el, 1)

            def att_before(b):
                return not isinstance(b, int) or b >= 1

            def body(b, par, att, pre, post):
                A = b - 1
                for h in range(NH):
                    for t in range(NT):
                        p = h * NT + t
                        if p - 1 in UNITS:
                            name = UNITS[p - 1]
                            if name[0] in "ZGR":
                                pass
                            elif has(b, name, att, pre, post):
                                evacuate(b, par, name)
                            else:
                                act.wait_ge(g_full, unit(b, name) + 1)
                                if name in HI:
                                    act.wait_ge(g_hi, hi_index(b, name))
                                else:
                                    act.wait_ge(g_free, unit(b, name))
                                act.nop().then_inc(g_hi if name in HI else g_free, 1)
                        if att:
                            n = b * POS + p
                            act.wait_ge(t_full, n + 1)
                            if not isinstance(b, int) or b > 0 or p >= 4:
                                act.wait_ge(p_lo, n - 3)
                            act.activation(pf[p % 4][:, :], T[p % 2][:, :], ACT.Exp, scale=SCALE).then_inc(p_exp, 1)
                        eb, ep, was = behind(b, p, 1, att)
                        if was and ep not in HIGH_ON_DVE:
                            n = eb * POS + ep
                            act.wait_ge(p_exp, n + 1)
                            act.wait_ge(p_hi, n)
                            if not isinstance(eb, int) or eb > 0 or ep >= 4:
                                act.wait_ge(pv, n - 3)
                            act.activation(ph[ep % 4][:, :], pf[ep % 4][:, :], ACT.Copy).then_inc(p_hi, 1)
                        if p == ACT_AT["tanh"] and post:
                            act.wait_ge(g_free, unit(b, "Z1") + 1)
                            act.activation(z[:, :, :], z[:, :, :], ACT.Tanh, scale=0.5).then_inc(s_z, 1)
                        if p == ACT_AT["exp"] and late(b):
                            second_choice(b - 2)
                        eb, ep, was = behind(b, p, NT + LAG - 1, att)
                        if was and t == (NT + LAG - 1) % NT:
                            eh = ep // NT
                            act.wait_ge(pv, eb * POS + eh * NT + NT)
                            if not (isinstance(eb, int) and eb == 0 and eh < 2):
                                act.wait_ge(b_full, eb * NH + eh - 1)
                            act.activation(ct[eh % 2][0:2 * DK + 1, :], C[0:2 * DK + 1, :], ACT.Copy).then_inc(s_ct, 1)
                        eb, ep, was = behind(b, p, 2 * NT + 1, att)
                        if was and t == 1:
                            eh = ep // NT
                            act.wait_ge(b_full, eb * NH + eh + 1)
                            if eh % 4 == 0:
                                act.wait_ge(s_norm, eb * 6)
                            act.activation(cb[:, eh, :, 0:2 * DK + 1],
                                           BT[:, 0:NT * VW].rearrange("p (i w) -> p i w", w=VW)[:, :, 0:2 * DK + 1],
                                           ACT.Copy).then_inc(b_free, 1)

            iterations(act, body)
            second_choice(NB - 1)

        @block.vector
        def _(dve):
            zf = z[:, :, :].rearrange("p i d -> p (i d)")
            df = diff[:, :, :].rearrange("p i d -> p (i d)")
            dve.memset(f32(stack[SR:SR + 2, :, 1, :]), 1.0).then_inc(s_set, 1)

            def prepare():
                for s in range(2):
                    for i in range(NT):
                        dve.memset(f32(v[s][:, i, :, 2 * DK:2 * DK + 2]), 1.0).then_inc(s_set, 1)
                dve.memset(msum[:, :], 0.0).then_inc(s_rt0, 1)
                dve.wait_ge(s_const, 9)
                dve.tensor_scalar(xn2[:, :, WT], tok_i[:, :], -float(N), None, ALU.add).then_inc(s_rt0, 1)
                dve.tensor_copy(iota_e[:, :], iota_i[:, :]).then_inc(s_rt0, 1)
                dve.wait_ge(s_rt0, 3)
                dve.tensor_scalar(start_e[:, :], iota_e[:, :], float(region), None, ALU.mult).then_inc(s_rt0, 1)
                dve.wait_ge(s_set, 12)
                dve.tensor_tensor(wqkv_l[:, 0, :], zf[:, 0:3 * D], f32(wqkv_h[:, 0, :]), ALU.subtract).then_inc(s_lo, 1)
                dve.tensor_tensor(wqkv_l[:, 1, :], df[:, 0:3 * D], f32(wqkv_h[:, 1, :]), ALU.subtract).then_inc(s_lo, 1)
                dve.tensor_tensor(wg_l[:, :, :], x1[:, :, :], f32(wg_h[:, :, :]), ALU.subtract).then_inc(s_lo, 1)
                dve.wait_ge(s_lo, 3)
                dve.wait_ge(s_rt0, 4)
                dve.nop().then_inc(s_set, 2)

            def low(b, par, name):
                B, A = b + 1, b - 1
                o = bank(par, name)
                k = int(name[1])
                if name[0] in "PQKVC":
                    dve.wait_ge(g_hi, hi_index(b, name) + 1)
                else:
                    dve.wait_ge(g_full, unit(b, name) + 1)
                dve.wait_ge(g_free, unit(b, name))
                if name[0] == "P":
                    dve.tensor_tensor(xt_l[:, k, :], o[:, :], f32(xt_h[:, k, :]), ALU.subtract).then_inc(g_free, 1)
                elif name[0] in "QK":
                    hi, lo = (QH, QL) if name[0] == "Q" else (KH, KL)
                    dve.tensor_tensor(qk[:, k, lo, :], o[:, :], f32(qk[:, k, hi, :]), ALU.subtract).then_inc(g_free, 1)
                elif name[0] == "V":
                    vv = v[par][:, 2 * k:2 * k + 2, :, :]
                    dve.tensor_tensor(vv[:, :, :, DK:2 * DK].rearrange("p i h d -> p (i h) d"),
                                      o[:, :].rearrange("p (j d) -> p j d", d=DK),
                                      f32(vv[:, :, :, 0:DK].rearrange("p i h d -> p (i h) d")),
                                      ALU.subtract).then_inc(g_free, 1)
                elif name[0] == "C":
                    dve.tensor_tensor(ct_l[:, k, :], o[:, :], f32(ct_h[:, k, :]), ALU.subtract).then_inc(g_free, 1)
                elif name[0] == "G":
                    dve.tensor_tensor(gx[1 - par][:, 2 * k:2 * k + 2, :], o[:, :].rearrange("p (i d) -> p i d", d=D),
                                      bgt[:, :].rearrange("p (o d) -> p o d", o=1).to_broadcast([P, 2, D]),
                                      ALU.add).then_inc(g_free, 1)
                elif name[0] == "Z":
                    dve.wait_ge(s_rt, A * RT)
                    dve.wait_ge(s_st, A * 32)
                    dve.tensor_tensor(z[:, 2 * k:2 * k + 2, :], o[:, :].rearrange("p (i d) -> p i d", d=D),
                                      gx[par][:, 2 * k:2 * k + 2, :], ALU.add).then_inc(g_free, 1)
                elif name[0] == "R":
                    dve.tensor_tensor(posb[:, :, :], o[:, 0:NT * E].rearrange("p (i e) -> p i e", e=E),
                                      start_e[:, :].rearrange("p (o e) -> p o e", o=1).to_broadcast([P, NT, E]),
                                      ALU.add).then_inc(g_free, 1)

            def skip(b, name):
                if name in HI:
                    dve.wait_ge(g_hi, hi_index(b, name) + 1)
                else:
                    dve.wait_ge(g_full, unit(b, name) + 1)
                dve.wait_ge(g_free, unit(b, name))
                dve.nop().then_inc(g_free, 1)

            def statistics(src, st, s, base):
                dve.wait_ge(s, base)
                for i in range(NT):
                    dve.bn_stats(st[:, i, :], src[:, i, :]).then_inc(s, 1)

            def variance(st, m, va, s, base):
                dve.wait_ge(s, base + NT)
                dve.nop().then_inc(s_held_dve, 1)
                for i in range(NT):
                    dve.bn_aggr(m[:, i, :], st[:, i, :]).then_inc(s, 1)
                dve.wait_ge(s, base + 2 * NT)
                dve.tensor_scalar(va[:, :], m[:, :, 1], LN_EPS, None, ALU.add).then_inc(s, 1)

            def normalise(half, b):
                hs = slice(4 * half, 4 * half + 4)
                base = b * 6 + 3 * half
                dve.wait_ge(b_free, b * NH + 4 * half + 4)
                dve.wait_ge(s_norm, base)
                dve.reciprocal(rden[:, hs, :], cb[:, hs, :, 2 * DK]).then_inc(s_norm, 1)
                cv = c_tok[:, :, :].rearrange("p i (h d) -> p h i d", d=DK)[:, hs]
                dve.tensor_tensor(cv, cb[:, hs, :, 0:DK], cb[:, hs, :, DK:2 * DK], ALU.add).then_inc(s_norm, 1)
                dve.wait_ge(s_norm, base + 2)
                dve.tensor_tensor(cv, cv, rden[:, hs, :].rearrange("p h (i o) -> p h i o", o=1)
                                  .to_broadcast([P, 4, NT, DK]), ALU.mult).then_inc(s_norm, 1)

            def choose(b, A):
                rt = A * RT
                dve.wait_ge(g_free, unit(b, "T0") + 1)
                dve.wait_ge(s_rt, rt)
                dve.nop().then_inc(s_held_dve, 1)
                for i in range(NT):
                    dve.max(mx8[:, i, :], lg[:, i, :]).then_inc(s_rt, 1)
                dve.wait_ge(s_rt, rt + RT_MAX)
                dve.nop().then_inc(s_held_dve, 1)
                for i in range(NT):
                    dve.max_index(ix8[:, i, :], mx8[:, i, :], lg[:, i, :]).then_inc(s_rt, 1)
                dve.wait_ge(s_rt, rt + RT_IX)
                dve.tensor_copy(ef[:, :, :], ix8[:, :, 0:2]).then_inc(s_rt, 1)

            def mark(A):
                rt = A * RT
                dve.wait_ge(s_rt, rt + RT_EF)
                oh = onehot[:, :, :]
                dve.tensor_tensor(oh, ef[:, :, :].rearrange("p i (k o) -> p (i k) o", o=1)
                                  .to_broadcast([P, 2 * NT, E]),
                                  iota_e[:, :].rearrange("p (o e) -> p o e", o=1)
                                  .to_broadcast([P, 2 * NT, E]), ALU.is_equal).then_inc(s_rt, 1)
                dve.wait_ge(s_rt, rt + RT_OH)
                ohk = oh.rearrange("p (i k) e -> p i k e", k=2)
                dve.tensor_tensor(mb[:, :, :], ohk[:, :, 0, :], ohk[:, :, 1, :], ALU.add).then_inc(s_rt, 1)
                dve.tensor_tensor(dl[:, :], mx8[:, :, 1], mx8[:, :, 0], ALU.subtract).then_inc(s_rt, 1)
                dve.wait_ge(s_rt, rt + RT_MB)
                dve.tensor_reduce(msd[:, :], mb[:, :, :].rearrange("p i e -> p e i"), AX_X,
                                  ALU.add).then_inc(s_rt, 1)

            def weigh(A):
                rt = A * RT
                wv = xn2[:, :, W0:W1 + 1]
                dve.wait_ge(s_el, A + 1)
                dve.wait_ge(s_scat, A * 16 * 2 * NT)
                dve.tensor_scalar(ea[:, :], el[:, :], 1.0, None, ALU.add).then_inc(s_rt, 1)
                dve.wait_ge(s_rt, rt + RT_EA)
                dve.reciprocal(wv[:, :, 0], ea[:, :]).then_inc(s_rt, 1)
                dve.wait_ge(s_rt, rt + RT_W0)
                dve.tensor_copy(xn2[:, :, WE], ef[:, :, 0]).then_inc(s_rt, 1)
                dve.tensor_scalar(xn2[:, :, WT], xn2[:, :, WT], float(N), None, ALU.add).then_inc(s_rt, 1)
                dve.tensor_tensor(wv[:, :, 1], el[:, :], wv[:, :, 0], ALU.mult).then_inc(s_rt, 1)

            def place(b, par):
                rt = (b - 2) * RT
                dve.wait_ge(g_full, unit(b, "R0") + 1)
                low(b, par, "R0")
                dve.tensor_tensor(msum[:, :], msum[:, :], msd[:, :], ALU.add).then_inc(s_rt, 1)
                dve.wait_ge(g_free, unit(b, "R0") + 1)
                oh = onehot[:, :, :].rearrange("p (i k) e -> p i k e", k=2)
                dve.tensor_tensor(pick[:, :, :, :], oh, posb[:, :, :].rearrange("p i (o e) -> p i o e", o=1)
                                  .to_broadcast([P, NT, 2, E]), ALU.mult).then_inc(s_rt, 1)
                dve.wait_ge(s_rt, rt + RT_PICK)
                sv = slot[:, :]
                dve.tensor_reduce(sv, pick[:, :, :, :].rearrange("p i k e -> p (i k) e"), AX_X,
                                  ALU.add).then_inc(s_rt, 1)
                dve.wait_ge(s_rt, rt + RT_SLOT)
                dve.tensor_copy(idx[:, :, :].rearrange("p i k -> p (i k)"), sv).then_inc(s_rt, 1)

            def body(b, par, att, pre, post):
                B, A = b + 1, b - 1
                for h in range(NH):
                    for t in range(NT):
                        p = h * NT + t
                        if p - 2 in UNITS:
                            name = UNITS[p - 2]
                            if name[0] in "PQKVCGZ" and has(b, name, att, pre, post):
                                low(b, par, name)
                            elif name[0] in "PQKVCGZ" or (name == "R0" and not late(b)):
                                skip(b, name)
                        eb, ep, was = behind(b, p, 1, att)
                        if was and ep in HIGH_ON_DVE:
                            n = eb * POS + ep
                            dve.wait_ge(p_exp, n + 1)
                            dve.wait_ge(p_hi, n)
                            if not isinstance(eb, int) or eb > 0 or ep >= 4:
                                dve.wait_ge(pv, n - 3)
                            dve.tensor_copy(ph[ep % 4][:, :], pf[ep % 4][:, :]).then_inc(p_hi, 1)
                        rb, rh, there = ahead(b, h - 1, att, pre)
                        if there and t == 0:
                            dve.wait_ge(s_full, (rb * NH + rh) * (NT + 1) + NT + 1)
                            if not (isinstance(rb, int) and rb == 0 and rh < 4):
                                fb = rb if rh >= 4 else rb - 1
                                dve.wait_ge(s_row[(rh - 4) % NH], fb * 16 + 16)
                            dve.tensor_copy(row[:, rh % 4, :], S[(rh * (NT + 1) + NT) % 2][0:2 * NT, 0:P]
                                            ).then_inc(s_done, 1)
                        gb, gh, there = ahead(b, h, att, pre)
                        if there:
                            gg = gb * NH + gh
                            slot2 = gh % 2
                            bq = bias_q[par if gh < AHEAD and h + AHEAD >= NH else 1 - par]
                            for i in {0: [0, 1], 1: [2, 3]}.get(t, []):
                                dve.wait_ge(s_full, gg * (NT + 1) + i + 1)
                                if i == 0 and gh == 0:
                                    dve.wait_ge(s_bias, gb * 2 + 2)
                                if i == 0 and not (isinstance(gb, int) and gb == 0 and gh < 2):
                                    dve.wait_ge(s_mcol, gg * 2 - 2)
                                o = S[(gh * (NT + 1) + i) % 2]
                                dve.nop().then_inc(s_held_dve, 1)
                                dve.tensor_tensor_reduce(o[:, :], o[:, :], bq[:, i, :], 1.0, 3.0 * MASKED,
                                                         ALU.add, ALU.max, mx[:, slot2, i:i + 1]).then_inc(s_done, 1)
                            if t == 2:
                                dve.wait_ge(s_done, gg * (NT + 1) + NT)
                                if not (isinstance(gb, int) and gb == 0 and gh < 2):
                                    dve.wait_ge(s_done, (gg - 1) * (NT + 1))
                                mc = mcol[:, slot2]
                                dve.tensor_scalar(mc[:, 0, :].bitcast(F32R), mx[:, slot2, :], -1.0, None,
                                                  ALU.mult).then_inc(s_mcol, 1)
                                dve.wait_ge(s_mcol, gg * 2 + 1)
                                dve.scalar_tensor_tensor(out=mc[:, 1, :], in0=mx[:, slot2, :], scalar=-1.0,
                                                         in1=mc[:, 0, :], op0=ALU.mult,
                                                         op1=ALU.subtract).then_inc(s_mcol, 1)
                        if pre and p == DVE_AT["stat"]:
                            dve.wait_ge(s_x, B * 16 + 16)
                            statistics(xn, stats, s_stat, B * (2 * NT + 1))
                        if pre and p == DVE_AT["var"]:
                            dve.wait_ge(s_xn, B * NT)
                            variance(stats, mv, vr, s_stat, B * (2 * NT + 1))
                        if pre and p in (DVE_AT["xn0"], DVE_AT["xn1"]):
                            dve.wait_ge(s_rstd, B + 1)
                            for i in ([0, 1] if p == DVE_AT["xn0"] else [2, 3]):
                                dve.tensor_scalar(xn[:, i, :], xn[:, i, :], mv[:, i, 0:1], rstd[:, i:i + 1],
                                                  ALU.subtract, ALU.mult).then_inc(s_xn, 1)
                        if isinstance(b, int) and b == -1 and p == UNIT_AT["P1"] + 2:
                            prepare()
                        if p == DVE_AT["norm1"] and ((0 < b <= NB) if isinstance(b, int) else True):
                            normalise(1, A)
                        if p == DVE_AT["norm0"] and att:
                            if post:
                                dve.wait_ge(s_d, A * 2 + 2)
                                dve.wait_ge(g_full, unit(b, "C1") + 1)
                            normalise(0, b)
                        if pre and p in (DVE_AT["bias0"], DVE_AT["bias1"]):
                            k = 0 if p == DVE_AT["bias0"] else 1
                            dve.wait_ge(s_adj, B * 32 + 16 * k + 16)
                            if not isinstance(b, int) or b >= 1:
                                dve.wait_ge(s_done, b * NH * (NT + 1))
                            dve.tensor_scalar(bias_q[par][:, 2 * k:2 * k + 2, :], adj_i[:, :, :], 0.0, MASKED,
                                              ALU.is_equal, ALU.mult).then_inc(s_bias, 1)
                        if post and p == DVE_AT["gate"]:
                            dve.wait_ge(s_z, A + 1)
                            dve.wait_ge(s_d, A * 2 + 2)
                            dve.scalar_tensor_tensor(out=df[:, :], in0=zf[:, :], scalar=1.0, in1=df[:, :],
                                                     op0=ALU.add, op1=ALU.mult).then_inc(s_mix, 1)
                        if post and p == DVE_AT["x1"]:
                            dve.wait_ge(s_mix, A * 2 + 1)
                            x1f = x1[:, :, :].rearrange("p i d -> p (i d)")
                            dve.scalar_tensor_tensor(out=x1f, in0=df[:, :], scalar=0.5, in1=x1f,
                                                     op0=ALU.mult, op1=ALU.add).then_inc(s_mix, 1)
                        if post and p == DVE_AT["stat2"]:
                            dve.wait_ge(s_mix, A * 2 + 2)
                            statistics(x1, stats2, s_stat2, A * (2 * NT + 1))
                        if post and p == DVE_AT["var2"]:
                            dve.wait_ge(s_xn2, A * NT)
                            variance(stats2, mv2, vr2, s_stat2, A * (2 * NT + 1))
                        if post and p == DVE_AT["xn2"]:
                            dve.wait_ge(s_rstd2, A + 1)
                            dve.wait_ge(s_scat, A * 16 * 2 * NT)
                            dve.wait_ge(s_st, A * 32)
                            for i in range(NT):
                                dve.tensor_scalar(xn2[:, i, 0:D], x1[:, i, :], mv2[:, i, 0:1], rstd2[:, i:i + 1],
                                                  ALU.subtract, ALU.mult).then_inc(s_xn2, 1)
                        if post and p == DVE_AT["choose"]:
                            choose(b, A)
                        if late(b) and p == DVE_AT["mark"]:
                            mark(b - 2)
                        if late(b) and p == DVE_AT["weigh"]:
                            weigh(b - 2)
                        if late(b) and p == DVE_AT["place"]:
                            place(b, par)

            iterations(dve, body)
            mark(NB - 1)
            weigh(NB - 1)
            place(NB + 1, NB % 2)

        @block.gpsimd
        def _(pool):
            for m in (ident, ident_b):
                pool.memset(m[:, :], 0.0).then_inc(s_const, 1)
            pool.memset(below[:, :], 1.0).then_inc(s_const, 1)
            pool.memset(ones_b[:, :], 1.0).then_inc(s_const, 1)
            pool.memset(mhalf[:, :], -0.5).then_inc(s_half, 1)
            pool.wait_ge(s_const, 4)
            for m in (ident, ident_b):
                pool.affine_select(out=m[:, :], in_=m[:, :], compare_op=ALU.not_equal, fill=1.0, base=0,
                                   pattern=[[-1, P]], channel_multiplier=1).then_inc(s_const, 1)
            pool.affine_select(out=below[:, :], in_=below[:, :], compare_op=ALU.is_gt, fill=0.0, base=0,
                               pattern=[[1, P]], channel_multiplier=-1).then_inc(s_const, 1)
            pool.iota(iota_i[:, :], [[1, E]], base=0, channel_multiplier=0).then_inc(s_const, 1)
            pool.iota(tok_i[:, :], [[P, NT]], base=0, channel_multiplier=1).then_inc(s_const, 1)
            pool.wait_ge(s_half, 1)

            def scatter(A, j):
                if j == 0:
                    pool.wait_ge(s_rt, A * RT + RT_IDX)
                    pool.nop().then_inc(s_held_pool, 1)
                i, k = j // 2, j % 2
                pool.indirect_dma_start(
                    out=xg_dram, out_offset=bass.IndirectOffsetOnAxis(ap=idx[:, i, k:k + 1], axis=0),
                    in_=xn2[:, i, :], in_offset=None).then_inc(s_scat, 16)

            def body(b, par, att, pre, post):
                B, A = b + 1, b - 1
                for p in range(POS):
                    if (b >= 2 if isinstance(b, int) else True) and 0 <= p - POOL_AT["scatter"] < 2 * NT:
                        scatter(b - 2, p - POOL_AT["scatter"])
                    if pre and p == POOL_AT["rstd"]:
                        pool.wait_ge(s_stat, B * (2 * NT + 1) + 2 * NT + 1)
                        pool.wait_ge(s_xn, B * NT)
                        pool.tensor_tensor(rstd[:, :], vr[:, :], mhalf[:, :], ALU.pow).then_inc(s_rstd, 1)
                    if post and p in (POOL_AT["diff"], POOL_AT["x1"]):
                        pool.wait_ge(s_norm, A * 6 + 6)
                        pool.wait_ge(s_xp, A * 32 + 32)
                        if p == POOL_AT["diff"]:
                            pool.wait_ge(g_free, (b) * NU)
                            pool.tensor_tensor(diff[:, :, :], xnp[:, :, :], c_tok[:, :, :], ALU.subtract).then_inc(s_d, 1)
                        else:
                            pool.wait_ge(s_st, A * 32)
                            pool.wait_ge(s_xn2, A * NT)
                            pool.tensor_tensor(x1[:, :, :], xp[:, :, :], c_tok[:, :, :], ALU.add).then_inc(s_d, 1)
                    if post and p == POOL_AT["rstd2"]:
                        pool.wait_ge(s_stat2, A * (2 * NT + 1) + 2 * NT + 1)
                        pool.tensor_tensor(rstd2[:, :], vr2[:, :], mhalf[:, :], ALU.pow).then_inc(s_rstd2, 1)
                    if att:
                        n = b * POS + p
                        pool.wait_ge(p_hi, n + 1)
                        if not isinstance(b, int) or b > 0 or p >= 4:
                            pool.wait_ge(pv, n - 3)
                        pool.tensor_tensor(pl[p % 4][:, :], pf[p % 4][:, :], f32(ph[p % 4][:, :]),
                                           ALU.subtract).then_inc(p_lo, 1)
            iterations(pool, body)


def ffn_phase(nc, sems, w_dram, xt2_dram, x1_dram, xg_dram, out, ident, msum, xn2, idx, s_scat, nb, region,
              experts, inter):
    D = out.shape[1]
    TOKENS = nb * BLOCK
    KF = D // P
    MT = inter // P
    NT = BLOCK // P
    SH = nb
    NR = (2 * TOKENS + experts * (BLOCK - 1)) // BLOCK
    NBLK = SH + NR
    GU = 2 * KF * inter
    WC = GU + MT * D
    CH = WC // 3
    assert CH == KF * inter == MT * D
    assert SH % 2 == 0 and NR % 2 == 1
    MAXB = TOKENS // BLOCK
    W0, W1, WE, WT = D, D + 1, D + 2, D + 3
    UNUSED = experts * region

    ctx = ExitStack()
    with ctx:
        def sb(name, shape, dt=F32):
            return ctx.enter_context(nc.sbuf_tensor(name, shape, dt))

        def sem(name):
            return sems.enter_context(nc.semaphore(name))

        banks = [ctx.enter_context(nc.psum_tensor(f"fbank{i}", [P, 512], F32)) for i in range(8)]
        GB, UB, TB, OB = banks[0:2], banks[2:4], banks[4:6], banks[6:8]

        raw = [sb(f"raw{s}", [P, WC]) for s in range(2)]
        wh = [sb(f"wh{s}", [P, WC], F32R) for s in range(2)]
        wl = [sb(f"wl{s}", [P, WC], F32R) for s in range(2)]
        xb = [sb(f"xb{s}", [P, NT, XW]) for s in range(2)]
        x1b = [sb(f"x1b{s}", [P, NT, D]) for s in range(2)]
        xh = [sb(f"xh{s}", [P, KF, BLOCK], F32R) for s in range(2)]
        xl = [sb(f"xl{s}", [P, KF, BLOCK], F32R) for s in range(2)]
        sg = [sb(f"sg{s}", [P, BLOCK]) for s in range(2)]
        am = [sb(f"am{s}", [P, BLOCK]) for s in range(2)]
        ah = [sb(f"ah{s}", [P, MT, BLOCK], F32R) for s in range(2)]
        al = [sb(f"al{s}", [P, MT, BLOCK], F32R) for s in range(2)]
        yb = [sb(f"yb{s}", [P, NT, D]) for s in range(2)]
        fones = sb("fones", [P, P], BF16)
        pad = sb("pad", [P, NT, XW])
        padi = sb("padi", [P, NT], I32)
        cnt = sb("cnt", [P, experts])
        ki = sb("ki", [P, MAXB], I32)
        kf_ = sb("kf_", [P, MAXB])
        cmp = sb("cmp", [P, experts, MAXB])
        nblk = sb("nblk", [P, experts])
        ones_e = sb("ones_e", [P, experts])
        cum = sb("cum", [P, experts])
        base = sb("base", [P, experts])
        ei = sb("ei", [P, experts], I32)
        ef = sb("eft", [P, experts])
        est = sb("est", [P, experts])
        shift = sb("shift", [P, experts])
        ji = sb("ji", [P, NR], I32)
        jf = sb("jf", [P, NR])
        ge0 = sb("ge0", [P, NR, experts])
        ge1 = sb("ge1", [P, NR, experts])
        jr = sb("jr", [P, NR])
        rows = sb("rows", [P, NR, experts])
        tef = sb("tef", [P, NR])
        trf = sb("trf", [P, NR])
        tab_e = sb("tab_e", [P, NR], I32)
        tab_r = sb("tab_r", [P, NR], I32)
        toff = sb("toff", [P, experts, NT], I32)
        tofff = sb("tofff", [P, experts, NT])
        tstart = sb("tstart", [P, experts])
        tidx = sb("tidx", [P, experts, NT], U32)
        own = sb("own", [P, 1])
        wa = sb("wa", [P, NT])
        wb = sb("wb", [P, NT])
        wt = [sb(f"wt{s}", [P, NT]) for s in range(2)]
        ix = [sb(f"ix{s}", [P, NT], U32) for s in range(2)]

        s_ones = sem("s_ones")
        s_k = sem("s_k")
        s_cnt = sem("s_cnt")
        s_tb = sem("s_tb")
        s_pad = sem("s_pad")
        s_tail = sem("s_tail")
        s_raws = [sem(f"s_raws{t}") for t in range(3)]
        s_raw = [sem(f"s_raw{s}") for s in range(2)]
        s_xb = [sem(f"s_xb{s}") for s in range(2)]
        s_x1b = [sem(f"s_x1b{s}") for s in range(2)]
        s_yb = [sem(f"s_yb{s}") for s in range(2)]
        s_acc = sem("s_acc")
        s_wh = sem("s_wh")
        s_wl = sem("s_wl")
        s_tk = sem("s_tk")
        x_full = sem("x_full")
        x_hi = sem("x_hi")
        x_lo = sem("x_lo")
        g_full = sem("g_fullb")
        u_full = sem("u_full")
        s_sg = sem("s_sg")
        s_am = sem("s_am")
        s_ah = sem("s_ah")
        s_al = sem("s_al")
        y_full = sem("y_full")
        s_y = [sem(f"s_y{j}") for j in range(2)]

        s_held_dve, s_held_pool, s_held_sp = (sem(f"f_held_{e}") for e in ("dve", "pool", "sp"))

        block = ctx.enter_context(nc.Block())
        TB_N = 14
        TK = 5
        SW = 1

        def blocks(eng, body):
            body(0, 0, True, None, True)
            body(1, 1, True, True, True)
            body(2, 0, True, True, True)
            with eng.Fori(1, (SH - 2) // 2) as i:
                body(i * 2 + 1, 1, True, True, True)
                body(i * 2 + 2, 0, True, True, True)
            body(SH - 1, 1, True, True, False)
            body(SH, 0, False, True, False)
            body(SH + 1, 1, False, False, False)
            with eng.Fori(SH // 2 + 1, (NBLK - 1) // 2) as i:
                body(i * 2, 0, False, False, False)
                body(i * 2 + 1, 1, False, False, False)
            body(NBLK - 1, 0, False, False, None)

        def flat(s):
            return xb[s][:, :, :].rearrange("p i w -> p (i w)")[:, 0:KF * BLOCK]

        def parts(n, shared):
            return 0 if shared else (n - SH) * 3 + 3

        def wslot(s, shared):
            return SW if shared else s

        @block.gpsimd
        def _(pool):
            pool.memset(fones[:, :], 1.0).then_inc(s_ones, 1)
            pool.iota(ki[:, :], [[BLOCK, MAXB]], base=0, channel_multiplier=0).then_inc(s_k, 1)
            pool.iota(ei[:, :], [[1, experts]], base=0, channel_multiplier=0).then_inc(s_k, 1)
            pool.iota(ji[:, :], [[1, NR]], base=0, channel_multiplier=0).then_inc(s_k, 1)
            pool.iota(toff[:, :, :], [[0, experts], [P, NT]], base=0, channel_multiplier=1).then_inc(s_k, 1)
            pool.iota(padi[:, :], [[P, NT]], base=TOKENS, channel_multiplier=1).then_inc(s_k, 1)

            def low(s, part, before):
                pool.wait_ge(s_wh, before + part + 1)
                c = slice(CH * part, CH * part + CH)
                pool.tensor_tensor(wl[s][:, c], raw[s][:, c], f32(wh[s][:, c]), ALU.subtract).then_inc(s_wl, 1)

            for part in range(3):
                low(SW, part, 0)
            for j in range(2 * NT):
                pool.indirect_dma_start(
                    out=xg_dram, out_offset=bass.IndirectOffsetOnAxis(ap=idx[:, j // 2, j % 2:j % 2 + 1], axis=0),
                    in_=xn2[:, j // 2, :], in_offset=None).then_inc(s_scat, 16)
            pool.wait_ge(s_tb, TB_N)
            for e in range(experts):
                for q in range(NT):
                    pool.indirect_dma_start(
                        out=xg_dram, out_offset=bass.IndirectOffsetOnAxis(ap=tidx[:, e, q:q + 1], axis=0),
                        in_=pad[:, q, :], in_offset=None).then_inc(s_tail, 16)

            def add(n, s, first):
                for j in range(2):
                    pool.wait_ge(s_y[j], n + 1)
                if first:
                    for t in range(2):
                        pool.wait_ge(s_yb[t], SH // 2 * 16)
                    pool.wait_ge(s_pad, 32)
                else:
                    pool.wait_ge(s_acc, (n - SH) * NT * 16)
                pool.nop().then_inc(s_held_pool, 1)
                for i in range(NT):
                    pool.indirect_dma_start(
                        out=out, out_offset=bass.IndirectOffsetOnAxis(ap=ix[s][:, i:i + 1], axis=0),
                        in_=yb[s][:, i, :], in_offset=None, compute_op=ALU.add).then_inc(s_acc, 16)

            def body(n, s, shared, before, after):
                if after is False:
                    for part in range(3):
                        low(1 - s, part, parts(n + 1, False))
                if before is False:
                    add(n - 1, 1 - s, isinstance(n, int) and n == SH + 1)

            blocks(pool, body)
            add(NBLK - 1, (NBLK - 1) % 2, False)
            pool.wait_ge(s_acc, NR * NT * 16)

        @block.sync
        def _(sp):
            def run_of(t, n):
                return (t[n * BLOCK:n * BLOCK + BLOCK] if isinstance(n, int) else
                        t[bass.ds(n * BLOCK, BLOCK)]).rearrange("(i p) d -> p i d", i=NT)

            def load_shared(n, s):
                sp.dma_start(flat(s), xt2_dram[n] if isinstance(n, int) else
                             xt2_dram[bass.ds(n, 1)].rearrange("o p c -> p (o c)")).then_inc(s_xb[s], 16)

            def load_x1(n, s):
                sp.dma_start(x1b[s][:, :, :], run_of(x1_dram, n)).then_inc(s_x1b[s], 16)

            def load_weights(n, s):
                r = n - SH
                e = sp.value_load(tab_e[0:1, r:r + 1] if isinstance(r, int) else tab_e[0:1, bass.ds(r, 1)],
                                  min_val=0, max_val=experts - 1)
                sp.dma_start(raw[s][:, :], w_dram[bass.ds(e, 1)].rearrange("o p c -> p (o c)")).then_inc(s_raw[s], 16)

            def load_routed(n, s):
                r = n - SH
                row = sp.value_load(tab_r[0:1, r:r + 1] if isinstance(r, int) else tab_r[0:1, bass.ds(r, 1)],
                                    min_val=0, max_val=UNUSED)
                sp.dma_start(xb[s][:, :, :], xg_dram[bass.ds(row, BLOCK)].rearrange("(p i) d -> p i d", i=NT)
                             ).then_inc(s_xb[s], 16)

            load_shared(0, 0)
            for part in range(3):
                c = slice(CH * part, CH * part + CH)
                sp.dma_start(raw[SW][:, c], w_dram[experts, :, c]).then_inc(s_raws[part], 16)
            load_shared(1, 1)
            load_x1(0, 0)
            load_x1(1, 1)

            def body(n, s, shared, before, after):
                if before is None:
                    return
                if after is False:
                    if isinstance(n, int) and n == SH - 1:
                        sp.wait_ge(s_tb, TB_N)
                    if isinstance(n, int) and n <= SH:
                        sp.wait_ge(s_wl, 3)
                    else:
                        sp.wait_ge(s_wl, parts(n - 1, False) + 3)
                    load_weights(n + 1, 1 - s)
                if after is not None:
                    if before:
                        sp.wait_ge(x_lo, n * KF)
                    else:
                        sp.wait_ge(x_full, (n - SH) * KF)
                    sp.nop().then_inc(s_held_sp, 1)
                    if after:
                        load_shared(n + 1, 1 - s)
                    else:
                        if isinstance(n, int) and n == SH - 1:
                            sp.wait_ge(s_scat, nb * 2 * NT * 16)
                            sp.wait_ge(s_tail, experts * NT * 16)
                            sp.wait_ge(s_pad, 32)
                        if not before:
                            sp.wait_ge(s_tk, (n - SH) * TK)
                            sp.nop().then_inc(s_held_sp, 1)
                        load_routed(n + 1, 1 - s)
                if isinstance(n, int) and n == 1:
                    sp.wait_ge(s_tb, TB_N)
                    sp.dma_start(out[TOKENS:TOKENS + BLOCK].rearrange("(q p) d -> p q d", p=P),
                                 pad[:, :, 0:D]).then_inc(s_pad, 16)
                    sp.dma_start(xg_dram[UNUSED:UNUSED + BLOCK].rearrange("(q p) d -> p q d", p=P),
                                 pad[:, :, :]).then_inc(s_pad, 16)
                if before:
                    for j in range(2):
                        sp.wait_ge(s_y[j], n)
                    sp.dma_start(run_of(out, n - 1), yb[1 - s][:, :, :]).then_inc(s_yb[1 - s], 16)
                    if after:
                        load_x1(n + 1, 1 - s)

            blocks(sp, body)
            for t in range(2):
                sp.wait_ge(s_yb[t], SH // 2 * 16)

        @block.tensor
        def _(pe):
            def turn(n, s):
                pe.wait_ge(s_xb[s], (n - s) * 8 + 16)
                for k in range(KF):
                    if not isinstance(n, int) or n > SH:
                        pe.wait_ge(x_lo, n * 2 + k - 1)
                    for i in range(NT):
                        last = pe.transpose(TB[k][:, P * i:P * i + P], xb[s][:, i, P * k:P * k + P], ident[:, :])
                    last.then_inc(x_full, 1)

            def split(out_, lh, ll, rh, rl, first, last):
                pe.matmul(out_, lh, rh, start=first, stop=False)
                pe.matmul(out_, lh, rl, start=False, stop=False)
                return pe.matmul(out_, ll, rh, start=False, stop=last)

            def gate_up(n, s, m, shared):
                ws = wslot(s, shared)
                if m == 0:
                    pe.wait_ge(x_lo, n * 2 + 2)
                k0 = n * MT + m
                for w, (bank, free, full) in enumerate([(GB, s_sg, g_full), (UB, s_am, u_full)]):
                    if m == 0:
                        pe.wait_ge(s_wl, parts(n, shared) + 1 + w)
                    if not (isinstance(k0, int) and k0 < 2):
                        pe.wait_ge(free, k0 - 1)
                    for k in range(KF):
                        c = CH * w + inter * k + P * m
                        last = split(bank[m % 2][:, :], wh[ws][:, c:c + P], wl[ws][:, c:c + P],
                                     xh[s][:, k, :], xl[s][:, k, :], k == 0, k == KF - 1)
                    last.then_inc(full, 1)

            def down(n, s, shared):
                ws = wslot(s, shared)
                pe.wait_ge(s_wl, parts(n, shared) + 3)
                pe.wait_ge(s_al, n * MT + MT)
                for j in range(2):
                    if isinstance(n, int) and n == 0:
                        pe.wait_ge(s_tb, 1)
                    else:
                        pe.wait_ge(s_y[j], n)
                    for ii in range(2):
                        i = 2 * j + ii
                        for m in range(MT):
                            c = 2 * CH + D * m
                            last = split(OB[j][:, D * ii:D * ii + D], ah[s][:, m, P * i:P * i + P],
                                         al[s][:, m, P * i:P * i + P], wh[ws][:, c:c + D], wl[ws][:, c:c + D],
                                         m == 0, m == MT - 1)
                    last.then_inc(y_full, 1)

            pe.wait_ge(s_ones, 1)
            pe.matmul(OB[0][:, 0:experts], fones[:, :], msum[:, :], start=True, stop=True).then_inc(s_cnt, 1)

            def body(n, s, shared, before, after):
                gate_up(n, s, 0, shared)
                gate_up(n, s, 1, shared)
                if before is not None:
                    down(n - 1, 1 - s, before)
                gate_up(n, s, 2, shared)
                if after is False:
                    turn(n + 1, 1 - s)
                gate_up(n, s, 3, shared)

            blocks(pe, body)
            down(NBLK - 1, 0, False)

        @block.scalar
        def _(act):
            def high(n, s, shared):
                if shared:
                    act.wait_ge(s_xb[s], (n - s) * 8 + 16)
                    if not isinstance(n, int) or n >= 2:
                        act.wait_ge(u_full, (n - 1) * MT)
                for k in range(KF):
                    if not shared:
                        act.wait_ge(x_full, (n - SH) * 2 + k + 1)
                    act.activation(xh[s][:, k, :], flat(s)[:, BLOCK * k:BLOCK * k + BLOCK] if shared else TB[k][:, :],
                                   ACT.Copy).then_inc(x_hi, 1)

            def out_(n, s, first):
                act.wait_ge(s_tk, (n - SH) * TK + TK)
                if first:
                    act.wait_ge(s_yb[s], SH // 2 * 16)
                else:
                    act.wait_ge(s_acc, (n - 1 - SH) * NT * 16)
                for j in range(2):
                    act.wait_ge(y_full, n * 2 + j + 1)
                    for ii in range(2):
                        i = 2 * j + ii
                        last = act.activation(yb[s][:, i, :], OB[j][:, D * ii:D * ii + D], ACT.Copy,
                                              scale=wt[s][:, i:i + 1])
                    last.then_inc(s_y[j], 1)

            def silu(n, s, m):
                k0 = n * MT + m
                act.wait_ge(g_full, k0 + 1)
                if not (isinstance(k0, int) and k0 < 2):
                    act.wait_ge(s_am, k0 - 1)
                act.activation(sg[m % 2][:, :], GB[m % 2][:, :], ACT.Silu).then_inc(s_sg, 1)
                act.wait_ge(s_am, k0 + 1)
                act.activation(ah[s][:, m, :], am[m % 2][:, :], ACT.Copy).then_inc(s_ah, 1)

            high(0, 0, True)

            def body(n, s, shared, before, after):
                silu(n, s, 0)
                silu(n, s, 1)
                if before is False:
                    out_(n - 1, 1 - s, isinstance(n, int) and n <= SH + 2)
                silu(n, s, 2)
                if after is not None:
                    high(n + 1, 1 - s, after)
                silu(n, s, 3)

            blocks(act, body)
            out_(NBLK - 1, 0, False)

        @block.vector
        def _(dve):
            step = [0]

            def chain(ins):
                step[0] += 1
                ins.then_inc(s_tb, 1)
                dve.wait_ge(s_tb, step[0])

            def over(a, shape, pattern):
                return a.rearrange(pattern, o=1).to_broadcast(shape)

            def high(s, part):
                c = slice(CH * part, CH * part + CH)
                dve.tensor_copy(wh[s][:, c], raw[s][:, c]).then_inc(s_wh, 1)

            def high_routed(n, s, part):
                dve.wait_ge(s_raw[s], (n - SH - s) * 8 + 16)
                if not (isinstance(n, int) and n == SH):
                    if part < 2:
                        dve.wait_ge(u_full, (n - 1) * MT)
                    else:
                        dve.wait_ge(y_full, (n - 1) * 2)
                high(s, part)

            def low_x(n, s, shared):
                for k in range(KF):
                    dve.wait_ge(x_hi, n * 2 + k + 1)
                    dve.tensor_tensor(xl[s][:, k, :], flat(s)[:, BLOCK * k:BLOCK * k + BLOCK] if shared else
                                      TB[k][:, :], f32(xh[s][:, k, :]), ALU.subtract).then_inc(x_lo, 1)

            def mul(n, s, m):
                k0 = n * MT + m
                dve.wait_ge(u_full, k0 + 1)
                dve.wait_ge(s_sg, k0 + 1)
                if not (isinstance(k0, int) and k0 < 2):
                    dve.wait_ge(s_al, k0 - 1)
                dve.tensor_tensor(am[m % 2][:, :], sg[m % 2][:, :], UB[m % 2][:, :], ALU.mult).then_inc(s_am, 1)
                dve.wait_ge(s_ah, k0 + 1)
                dve.tensor_tensor(al[s][:, m, :], am[m % 2][:, :], f32(ah[s][:, m, :]), ALU.subtract).then_inc(s_al, 1)

            def out_shared(n, s):
                dve.wait_ge(s_x1b[s], (n - s) * 8 + 16)
                if not isinstance(n, int) or n >= 2:
                    dve.wait_ge(s_yb[s], (n - s) * 8)
                for j in range(2):
                    dve.wait_ge(y_full, n * 2 + j + 1)
                    dve.tensor_tensor(yb[s][:, 2 * j:2 * j + 2, :], OB[j][:, :].rearrange("p (i d) -> p i d", d=D),
                                      x1b[s][:, 2 * j:2 * j + 2, :], ALU.add).then_inc(s_y[j], 1)

            def take(n, s):
                r = n - SH
                t0 = r * TK
                dve.wait_ge(s_xb[s], (n - s) * 8 + 16)
                if not (isinstance(n, int) and n < SH + 2):
                    dve.wait_ge(s_acc, (r - 1) * NT * 16)
                if not (isinstance(n, int) and n == SH):
                    dve.wait_ge(s_tk, t0)
                dve.nop().then_inc(s_held_dve, 1)
                dve.tensor_copy(own[:, :], tef[:, r:r + 1] if isinstance(r, int) else tef[:, bass.ds(r, 1)]
                                ).then_inc(s_tk, 1)
                dve.tensor_copy(ix[s][:, :], xb[s][:, :, WT]).then_inc(s_tk, 1)
                dve.wait_ge(s_tk, t0 + 2)
                dve.scalar_tensor_tensor(out=wa[:, :], in0=xb[s][:, :, WE], scalar=own[:, 0:1], in1=xb[s][:, :, W0],
                                         op0=ALU.is_equal, op1=ALU.mult).then_inc(s_tk, 1)
                dve.scalar_tensor_tensor(out=wb[:, :], in0=xb[s][:, :, WE], scalar=own[:, 0:1], in1=xb[s][:, :, W1],
                                         op0=ALU.not_equal, op1=ALU.mult).then_inc(s_tk, 1)
                dve.wait_ge(s_tk, t0 + 4)
                dve.tensor_tensor(wt[s][:, :], wa[:, :], wb[:, :], ALU.add).then_inc(s_tk, 1)

            def count_blocks():
                dve.memset(pad[:, :, :], 0.0).then_inc(s_k, 1)
                dve.wait_ge(s_k, 6)
                dve.tensor_copy(kf_[:, :], ki[:, :]).then_inc(s_k, 1)
                dve.tensor_copy(ef[:, :], ei[:, :]).then_inc(s_k, 1)
                dve.tensor_copy(jf[:, :], ji[:, :]).then_inc(s_k, 1)
                dve.tensor_copy(tofff[:, :, :], toff[:, :, :]).then_inc(s_k, 1)
                dve.tensor_copy(pad[:, :, WT], padi[:, :]).then_inc(s_k, 1)
                dve.memset(ones_e[:, :], 1.0).then_inc(s_k, 1)
                dve.wait_ge(s_k, 12)
                dve.tensor_scalar(est[:, :], ef[:, :], float(region), None, ALU.mult).then_inc(s_k, 1)
                dve.tensor_scalar(jr[:, :], jf[:, :], float(BLOCK), None, ALU.mult).then_inc(s_k, 1)
                dve.wait_ge(s_k, 14)
                dve.wait_ge(s_cnt, 1)
                chain(dve.tensor_copy(cnt[:, :], OB[0][:, 0:experts]))
                chain(dve.tensor_tensor(cmp[:, :, :], over(cnt[:, :], [P, experts, MAXB], "p (e o) -> p e o"),
                                        over(kf_[:, :], [P, experts, MAXB], "p (o k) -> p o k"), ALU.is_gt))
                chain(dve.tensor_reduce(nblk[:, :], cmp[:, :, :], AX_X, ALU.add))
                chain(dve.tensor_tensor_scan(cum[:, :], ones_e[:, :], nblk[:, :], 0.0, ALU.mult, ALU.add))
                chain(dve.tensor_tensor(base[:, :], cum[:, :], nblk[:, :], ALU.subtract))
                chain(dve.scalar_tensor_tensor(out=shift[:, :], in0=base[:, :], scalar=float(BLOCK), in1=est[:, :],
                                               op0=ALU.mult, op1=ALU.subtract))

            def locate_blocks():
                jb = over(jf[:, :], [P, NR, experts], "p (j o) -> p j o")
                dve.tensor_tensor(ge0[:, :, :], jb, over(base[:, :], [P, NR, experts], "p (o e) -> p o e"),
                                  ALU.is_ge).then_inc(s_k, 1)
                chain(dve.tensor_tensor(ge1[:, :, :], jb, over(cum[:, :], [P, NR, experts], "p (o e) -> p o e"),
                                        ALU.is_ge))
                dve.wait_ge(s_k, 15)
                chain(dve.tensor_tensor(ge0[:, :, :], ge0[:, :, :], ge1[:, :, :], ALU.subtract))
                chain(dve.tensor_tensor(rows[:, :, :], over(jr[:, :], [P, NR, experts], "p (j o) -> p j o"),
                                        over(shift[:, :], [P, NR, experts], "p (o e) -> p o e"), ALU.subtract))

            def tables():
                dve.tensor_tensor(tstart[:, :], cnt[:, :], est[:, :], ALU.add).then_inc(s_k, 1)
                dve.tensor_scalar(trf[:, :], ge1[:, :, experts - 1], float(UNUSED), None, ALU.mult).then_inc(s_k, 1)
                chain(dve.tensor_tensor(rows[:, :, :], rows[:, :, :], ge0[:, :, :], ALU.mult))
                dve.tensor_tensor(ge1[:, :, :], ge0[:, :, :], over(ef[:, :], [P, NR, experts], "p (o e) -> p o e"),
                                  ALU.mult).then_inc(s_k, 1)
                dve.wait_ge(s_k, 18)
                dve.tensor_tensor(tofff[:, :, :], tofff[:, :, :],
                                  over(tstart[:, :], [P, experts, NT], "p (e o) -> p e o"), ALU.add).then_inc(s_k, 1)
                dve.tensor_reduce(tef[:, :], ge1[:, :, :], AX_X, ALU.add).then_inc(s_k, 1)
                chain(dve.tensor_reduce(jr[:, :], rows[:, :, :], AX_X, ALU.add))
                dve.wait_ge(s_k, 20)
                chain(dve.tensor_tensor(trf[:, :], trf[:, :], jr[:, :], ALU.add))
                chain(dve.tensor_copy(tab_r[:, :], trf[:, :]))
                dve.tensor_copy(tidx[:, :, :], tofff[:, :, :]).then_inc(s_k, 1)
                dve.wait_ge(s_k, 21)
                chain(dve.tensor_copy(tab_e[:, :], tef[:, :]))
                assert step[0] == TB_N, step

            def body(n, s, shared, before, after):
                if after is False:
                    high_routed(n + 1, 1 - s, 0)
                    high_routed(n + 1, 1 - s, 1)
                mul(n, s, 0)
                mul(n, s, 1)
                if isinstance(n, int) and n == 0:
                    locate_blocks()
                if isinstance(n, int) and n == 1:
                    tables()
                if after is False:
                    high_routed(n + 1, 1 - s, 2)
                if before:
                    out_shared(n - 1, 1 - s)
                mul(n, s, 2)
                if after is not None:
                    low_x(n + 1, 1 - s, after)
                if not shared:
                    take(n, s)
                mul(n, s, 3)

            count_blocks()
            for part in range(3):
                dve.wait_ge(s_raws[part], 16)
                high(SW, part)
                if part == 1:
                    low_x(0, 0, True)
            blocks(dve, body)


def f32(t):
    return t.bitcast(F32)


def program(nc, x, adj, wqkv, wgate, bg, router_w, w_all, out):
    nb, n, d = x.shape
    experts = router_w.shape[1]
    inter = w_all.shape[2] * P // (3 * d)
    tokens = nb * n
    region = tokens + BLOCK
    assert XW == d + 4 and n == BLOCK
    xn_dram = nc.dram_tensor("xn_dram", (tokens, d), F32, kind="Internal").ap()
    x1_dram = nc.dram_tensor("x1_dram", (tokens, d), F32, kind="Internal").ap()
    xt2_dram = nc.dram_tensor("xt2_dram", (nb, P, n * d // P), F32, kind="Internal").ap()
    xg_dram = nc.dram_tensor("xg_dram", (experts * region + BLOCK, XW), F32, kind="Internal").ap()

    with ExitStack() as ctx:
        def sb(name, shape, dt=F32):
            return ctx.enter_context(nc.sbuf_tensor(name, shape, dt))

        ident = sb("ident", [P, P])
        msum = sb("msum", [P, experts], BF16)
        xn2 = sb("xn2", [P, n // P, XW])
        idx = sb("idx", [P, n // P, 2], U32)
        s_scat = ctx.enter_context(nc.semaphore("s_scat"))
        attention_phase(nc, ctx, x, adj, wqkv, wgate, bg, router_w, xn_dram, x1_dram, xt2_dram, xg_dram,
                        ident, msum, xn2, idx, s_scat, region)
        ffn_phase(nc, ctx, w_all, xt2_dram, x1_dram, xg_dram, out, ident, msum, xn2, idx, s_scat, nb, region,
                  experts, inter)


def kernel(x, adj, L0_gnn_Wq, L0_gnn_Wk, L0_gnn_Wv, L0_gnn_Wg, L0_gnn_bg, L0_ffn_router_w,
           L0_ffn_Wg, L0_ffn_Wu, L0_ffn_Wd, L0_ffn_Sg, L0_ffn_Su, L0_ffn_Sd):
    import numpy as np
    import concourse.bacc as bacc
    from concourse.bass_utils import run_bass_kernel_spmd

    def rows(w):
        w = np.asarray(w)
        e, k, n = w.shape
        return w.reshape(e, k // P, P, n).transpose(0, 2, 1, 3).reshape(e, P, k // P * n)

    arrays = {
        "x": np.asarray(x),
        "adj": np.asarray(adj),
        "wqkv": np.concatenate([np.asarray(w).T for w in (L0_gnn_Wq, L0_gnn_Wk, L0_gnn_Wv)], axis=1),
        "wgate": np.asarray(L0_gnn_Wg).T,
        "bg": np.asarray(L0_gnn_bg),
        "router_w": np.asarray(L0_ffn_router_w),
        "w_all": np.concatenate([np.concatenate([rows(w), rows(np.asarray(s)[None])], axis=0) for w, s in (
            (L0_ffn_Wg, L0_ffn_Sg), (L0_ffn_Wu, L0_ffn_Su), (L0_ffn_Wd, L0_ffn_Sd))], axis=2),
    }
    nc = bacc.Bacc("TRN2", target_bir_lowering=False, num_devices=1)
    in_map, args = {}, []
    for name, a in arrays.items():
        a = np.ascontiguousarray(a)
        in_map[f"in_{name}"] = a
        args.append(nc.dram_tensor(f"in_{name}", a.shape, mybir.dt.from_np(a.dtype), kind="ExternalInput").ap())
    nb, n, d = arrays["x"].shape
    out = nc.dram_tensor("out_x", (nb * n + BLOCK, d), F32, kind="ExternalOutput").ap()
    program(nc, *args, out)
    r = run_bass_kernel_spmd(nc, [in_map], core_ids=[0])
    return r.results[0]["out_x"][:nb * n].reshape(nb, n, d)
```
